# Optimizing a Trainium2 kernel written in Bass

```python
import numpy as np
import jax
import jax.numpy as jnp

def _softmax(x, axis=-1):
    return jax.nn.softmax(x, axis=axis)

def _gelu(x):
    return jax.nn.gelu(x, approximate=True)

def _silu(x):
    return jax.nn.silu(x)

def _sigmoid(x):
    return jax.nn.sigmoid(x)

def _layernorm(x, axis=-1, eps=1e-05):
    m = jnp.mean(x, axis=axis, keepdims=True)
    v = jnp.var(x, axis=axis, keepdims=True)
    return (x - m) / jnp.sqrt(v + eps)

def _scatter_add(tgt, idx, src, axis=0):
    return tgt.at[idx].add(src)

def _segment_sum(src, seg, n):
    return jax.ops.segment_sum(src, seg, n)
kernel_name = 'mk_macaron_d1_jaxref_r8_a55335'

def setup_inputs(seed: int=0):
    np.random.seed(seed)
    _w = jnp.asarray

    def _L0_attn_setup():
        import math
        import jax, jax.numpy as jnp
        import numpy as np
        NUM_HEADS = 32
        HIDDEN = 512
        HEAD_DIM = HIDDEN // NUM_HEADS
        NEG_INF = -1e+30

        def _alibi_slopes(n: int) -> jnp.ndarray:
            cp2 = 2 ** math.floor(math.log2(n))
            base = 2.0 ** (-2.0 ** (-(math.log2(cp2) - 3)))
            slopes = base ** np.arange(1, cp2 + 1, dtype=np.float64)
            if cp2 != n:
                extra_base = 2.0 ** (-2.0 ** (-(math.log2(2 * cp2) - 3)))
                rem = min(cp2, n - cp2)
                extra = extra_base ** np.arange(1, 1 + 2 * rem, 2, dtype=np.float64)
                slopes = np.concatenate([slopes, extra])
            return jnp.asarray(slopes, dtype=jnp.float32)
        key = jax.random.key(seed)
        k1, k2, k3 = jax.random.split(key, 3)
        B, S = (2, 256)
        hidden_states = jax.random.normal(k1, (B, S, HIDDEN), dtype=jnp.float32)
        Wqkv = jax.random.normal(k2, (HIDDEN, NUM_HEADS * HEAD_DIM + 2 * HEAD_DIM), dtype=jnp.float32) * 0.02
        Wo = jax.random.normal(k3, (HIDDEN, HIDDEN), dtype=jnp.float32) * 0.02
        return {'hidden_states': hidden_states, 'Wqkv': Wqkv, 'Wo': Wo}
    _L0_attn_in = _L0_attn_setup()

    def _L0_ffn_setup():
        import jax, jax.numpy as jnp
        import numpy as np
        HIDDEN = 512
        INTER = 1376
        GROUP = 128
        B, S = (4, 256)
        NIB = jnp.uint32(15)

        def _pack_rows(nib):
            r = nib.reshape(-1, 8, nib.shape[-1])
            shifts = (jnp.arange(8, dtype=jnp.uint32) * 4)[None, :, None]
            return jnp.sum(r << shifts, axis=1, dtype=jnp.uint32)

        def _pack_cols(nib):
            r = nib.reshape(nib.shape[0], -1, 8)
            shifts = (jnp.arange(8, dtype=jnp.uint32) * 4)[None, None, :]
            return jnp.sum(r << shifts, axis=2, dtype=jnp.uint32)

        def _dequant(qw, qz, sc, g_idx):
            shifts = jnp.arange(8, dtype=jnp.uint32) * 4
            wq = qw[:, None, :] >> shifts[None, :, None] & NIB
            wq = wq.reshape(-1, qw.shape[1]).astype(jnp.float32)
            zq = qz[:, :, None] >> shifts[None, None, :] & NIB
            zq = zq.reshape(qz.shape[0], -1).astype(jnp.float32) + 1.0
            return sc[g_idx] * (wq - zq[g_idx])
        key = jax.random.key(seed)
        ks = jax.random.split(key, 7)
        n_groups = HIDDEN // GROUP
        n_groups_d = INTER // GROUP
        x = jax.random.normal(ks[0], (B, S, HIDDEN), jnp.float32)
        nib_w_gu = jax.random.randint(ks[1], (HIDDEN, 2 * INTER), 0, 16).astype(jnp.uint32)
        nib_z_gu = jax.random.randint(ks[2], (n_groups, 2 * INTER), 0, 15).astype(jnp.uint32)
        qweight_gu = _pack_rows(nib_w_gu)
        qzeros_gu = _pack_cols(nib_z_gu)
        scales_gu = jax.random.uniform(ks[3], (n_groups, 2 * INTER), jnp.float32, 0.005, 0.02)
        g_idx_gu = jnp.arange(HIDDEN, dtype=jnp.int32) // GROUP
        nib_w_d = jax.random.randint(ks[4], (INTER, HIDDEN), 0, 16).astype(jnp.uint32)
        nib_z_d = jax.random.randint(ks[5], (n_groups_d, HIDDEN), 0, 15).astype(jnp.uint32)
        qweight_down = _pack_rows(nib_w_d)
        qzeros_down = _pack_cols(nib_z_d)
        scales_down = jax.random.uniform(ks[6], (n_groups_d, HIDDEN), jnp.float32, 0.005, 0.02)
        g_idx_down = jnp.arange(INTER, dtype=jnp.int32) // GROUP
        return {'x': x, 'qweight_gu': qweight_gu, 'qzeros_gu': qzeros_gu, 'scales_gu': scales_gu, 'g_idx_gu': g_idx_gu, 'qweight_down': qweight_down, 'qzeros_down': qzeros_down, 'scales_down': scales_down, 'g_idx_down': g_idx_down}
    _L0_ffn_in = _L0_ffn_setup()
    _d = {'L0_attn_hidden_states': _L0_attn_in['hidden_states'], 'L0_attn_Wqkv': _L0_attn_in['Wqkv'], 'L0_attn_Wo': _L0_attn_in['Wo'], 'L0_ffn_qweight_gu': _L0_ffn_in['qweight_gu'], 'L0_ffn_qzeros_gu': _L0_ffn_in['qzeros_gu'], 'L0_ffn_scales_gu': _L0_ffn_in['scales_gu'], 'L0_ffn_g_idx_gu': _L0_ffn_in['g_idx_gu'], 'L0_ffn_qweight_down': _L0_ffn_in['qweight_down'], 'L0_ffn_qzeros_down': _L0_ffn_in['qzeros_down'], 'L0_ffn_scales_down': _L0_ffn_in['scales_down'], 'L0_ffn_g_idx_down': _L0_ffn_in['g_idx_down']}
    _x0 = _d['L0_attn_hidden_states']
    _d['L0_attn_hidden_states'] = jax.random.normal(jax.random.fold_in(jax.random.key(seed), 1), (4, 256, 512), dtype=_x0.dtype)
    del _x0
    return _d

def reference(L0_attn_hidden_states, L0_attn_Wqkv, L0_attn_Wo, L0_ffn_qweight_gu, L0_ffn_qzeros_gu, L0_ffn_scales_gu, L0_ffn_g_idx_gu, L0_ffn_qweight_down, L0_ffn_qzeros_down, L0_ffn_scales_down, L0_ffn_g_idx_down):

    def _L0_attn_ref(hidden_states, Wqkv, Wo):
        import math
        import jax, jax.numpy as jnp
        import numpy as np
        NUM_HEADS = 32
        HIDDEN = 512
        HEAD_DIM = HIDDEN // NUM_HEADS
        NEG_INF = -1e+30

        def _alibi_slopes(n: int) -> jnp.ndarray:
            cp2 = 2 ** math.floor(math.log2(n))
            base = 2.0 ** (-2.0 ** (-(math.log2(cp2) - 3)))
            slopes = base ** np.arange(1, cp2 + 1, dtype=np.float64)
            if cp2 != n:
                extra_base = 2.0 ** (-2.0 ** (-(math.log2(2 * cp2) - 3)))
                rem = min(cp2, n - cp2)
                extra = extra_base ** np.arange(1, 1 + 2 * rem, 2, dtype=np.float64)
                slopes = np.concatenate([slopes, extra])
            return jnp.asarray(slopes, dtype=jnp.float32)
        B, S, H = hidden_states.shape
        nH, d = (NUM_HEADS, HEAD_DIM)
        scale = d ** (-0.5)
        qkv = hidden_states @ Wqkv
        q = qkv[..., :nH * d].reshape(B, S, nH, d)
        k = qkv[..., nH * d:nH * d + d]
        v = qkv[..., nH * d + d:]
        scores = jnp.einsum('bqhd,bkd->bhqk', q, k) * scale
        pos_q = jnp.arange(S)[:, None]
        pos_k = jnp.arange(S)[None, :]
        slopes = _alibi_slopes(nH)
        alibi = slopes[:, None, None] * (pos_k - pos_q).astype(jnp.float32)
        causal = pos_k <= pos_q
        scores = jnp.where(causal[None, None], scores + alibi[None], NEG_INF)
        probs = jax.nn.softmax(scores, axis=-1)
        attn = jnp.einsum('bhqk,bkd->bqhd', probs, v).reshape(B, S, H)
        return attn @ Wo

    def _L0_ffn_ref(x, qweight_gu, qzeros_gu, scales_gu, g_idx_gu, qweight_down, qzeros_down, scales_down, g_idx_down):
        import jax, jax.numpy as jnp
        import numpy as np
        HIDDEN = 512
        INTER = 1376
        GROUP = 128
        B, S = (4, 256)
        NIB = jnp.uint32(15)

        def _pack_rows(nib):
            r = nib.reshape(-1, 8, nib.shape[-1])
            shifts = (jnp.arange(8, dtype=jnp.uint32) * 4)[None, :, None]
            return jnp.sum(r << shifts, axis=1, dtype=jnp.uint32)

        def _pack_cols(nib):
            r = nib.reshape(nib.shape[0], -1, 8)
            shifts = (jnp.arange(8, dtype=jnp.uint32) * 4)[None, None, :]
            return jnp.sum(r << shifts, axis=2, dtype=jnp.uint32)

        def _dequant(qw, qz, sc, g_idx):
            shifts = jnp.arange(8, dtype=jnp.uint32) * 4
            wq = qw[:, None, :] >> shifts[None, :, None] & NIB
            wq = wq.reshape(-1, qw.shape[1]).astype(jnp.float32)
            zq = qz[:, :, None] >> shifts[None, None, :] & NIB
            zq = zq.reshape(qz.shape[0], -1).astype(jnp.float32) + 1.0
            return sc[g_idx] * (wq - zq[g_idx])
        w_gu = _dequant(qweight_gu, qzeros_gu, scales_gu, g_idx_gu)
        inter = jnp.einsum('bsh,hf->bsf', x, w_gu)
        gate, up = (inter[..., :INTER], inter[..., INTER:])
        h = jax.nn.silu(gate) * up
        w_d = _dequant(qweight_down, qzeros_down, scales_down, g_idx_down)
        return jnp.einsum('bsf,fh->bsh', h, w_d)
    x = L0_attn_hidden_states
    x = x + 0.5 * _L0_ffn_ref(_layernorm(x, axis=-1), L0_ffn_qweight_gu, L0_ffn_qzeros_gu, L0_ffn_scales_gu, L0_ffn_g_idx_gu, L0_ffn_qweight_down, L0_ffn_qzeros_down, L0_ffn_scales_down, L0_ffn_g_idx_down)
    x = x + _L0_attn_ref(_layernorm(x, axis=-1), L0_attn_Wqkv, L0_attn_Wo)
    x = x + 0.5 * _L0_ffn_ref(_layernorm(x, axis=-1), L0_ffn_qweight_gu, L0_ffn_qzeros_gu, L0_ffn_scales_gu, L0_ffn_g_idx_gu, L0_ffn_qweight_down, L0_ffn_qzeros_down, L0_ffn_scales_down, L0_ffn_g_idx_down)
    return x

_drawn_inputs = setup_inputs


def setup_inputs(seed=0):
    import zlib

    import numpy as np

    out = dict(_drawn_inputs(seed))
    spreads = {}
    factors = {}
    for name, (base, spread) in spreads.items():
        noise = np.random.default_rng([zlib.crc32(name.encode()), seed]).standard_normal(out[name].shape)
        drawn = base * np.exp(spread * noise) if base else spread * noise
        out[name] = jnp.asarray(drawn.astype(out[name].dtype))
    for name, factor in factors.items():
        out[name] = (out[name] * factor).astype(out[name].dtype)
    return out
```

```python
from contextlib import ExitStack

import numpy as np

import concourse.bass as bass
from concourse import mybir

F32 = mybir.dt.float32
F32R = mybir.dt.float32r
BF16 = mybir.dt.bfloat16
I32 = mybir.dt.int32
U32 = mybir.dt.uint32
ALU = mybir.AluOpType
ACT = mybir.ActivationFunctionType
AX_X = mybir.AxisListType.X

P = 128
EPS = 1e-5


def alibi_slopes(n):
    cp2 = 2 ** int(np.floor(np.log2(n)))
    base = 2.0 ** (-2.0 ** (-(np.log2(cp2) - 3)))
    return [float(np.float32(v)) for v in base ** np.arange(1, n + 1, dtype=np.float64)]


class Steps:

    def __init__(self, eng, sem, base=0):
        self.eng, self.sem, self.base, self.n = eng, sem, base, 0

    def did(self, ins):
        ins.then_inc(self.sem, 1)
        self.n += 1

    def wait(self):
        self.eng.wait_ge(self.sem, self.base + self.n)


def macaron_block(nc, x_in, w_qkv, w_o, qw_gu, qz_gu, sc_gu, gi_gu, qw_d, qz_d, sc_d, gi_d, out):
    B, S, D = x_in.shape
    T = B * S
    HD = (w_qkv.shape[1] - D) // 2
    NH = D // HD
    F = qw_d.shape[0] * 8
    G_GU, G_D = sc_gu.shape[0], sc_d.shape[0]
    TT = T // P
    KT = D // P
    NJ = (F + P - 1) // P
    HALF = 4 * P
    NHALF = T // HALF
    JA = 6
    FA, FB = JA * P, F - JA * P
    NG = NH // 4
    SLOPES = alibi_slopes(NH)
    RC = 2 * F + D
    KC = D + F
    assert (D, HD, S, TT % 4, NHALF) == (512, 16, 2 * P, 0, 2)

    def jw(j):
        return min(P, F - j * P)

    x_tiles = x_in.rearrange("b (t p) d -> (b t) p d", p=P)
    out_tiles = out.rearrange("b (t p) d -> (b t) p d", p=P)
    spill = nc.dram_tensor("gate_up_tail", (P, 2 * KT * 2 * FB), F32, kind="Internal").ap()

    at = [(nc.sbuf_base + 31) // 32 * 32]

    def place(name, shape, dt, size):
        t = nc.alloc_sbuf_tensor_at(name, shape, dt, offset=at[0])
        n = int(np.prod(shape[1:])) * size
        at[0] += (n + 31) // 32 * 32
        return t

    x = place("x", [P, TT, D], F32, 4)
    w_a = place("w_a", [P, 2, KT, 2, FA], F32R, 4)
    w_d = place("w_d", [P, 2, NJ, D], F32R, 4)
    xt_at = at[0]
    xt = place("xt", [P, 2, KT, HALF], F32R, 4)
    xn = place("xn", [P, 2, D], F32, 4)
    ident = place("ident", [P, P], F32, 4)
    dist = place("dist", [P, 3, P], F32, 4)
    pid = place("pid", [P, 4], I32, 4)
    shifts = place("shifts", [P, 1], I32, 4)
    row32 = place("row32", [P, 1], F32, 4)
    headmask = place("headmask", [P, 4], F32, 4)
    hsel = place("hsel", [P, 1], F32, 4)
    stats = place("stats", [P, 6], F32, 4)
    mv = place("mv", [P, 4, 2], F32, 4)
    nwt = place("nwt", [P, 4, 4], F32, 4)
    nmax = place("nmax", [P, 2, 8], F32, 4)
    dq_at = at[0]
    table = place("table", [P, RC], BF16, 2)
    onehot = place("onehot", [P, KC], BF16, 2)
    raw = place("raw", [P, 4, 512], I32, 4)
    wf = place("wf", [P, 2, 512], F32, 4)
    ff_at = at[0]
    sil = place("sil", [P, 2, HALF], F32, 4)
    hf = place("hf", [P, 2, HALF], F32, 4)
    hs = place("hs", [P, 2, 2, HALF], F32R, 4)
    tail_at = at[0]
    w_b = place("w_b", [P, 2, KT, 2, FB], F32R, 4)
    top = at[0]
    at[0] = tail_at
    sraw = place("sraw", [P, RC], F32, 4)
    zint_at = at[0]
    zint = place("zint", [P, RC], I32, 4)
    zraw = place("zraw", [P, RC // 8], I32, 4)
    gint = place("gint", [P, KC], I32, 4)
    assert at[0] <= top
    at[0] = zint_at
    gflt = place("gflt", [P, KC], F32, 4)
    at[0] = dq_at
    wqkv = place("wqkv", [P, KT, D + 2 * HD], F32, 4)
    wo = place("wo", [P, KT, D], F32, 4)
    wk8 = place("wk8", [P, KT, P], F32, 4)
    wv4 = place("wv4", [P, KT, 4 * HD], F32, 4)
    assert at[0] <= ff_at
    at[0] = ff_at
    qp = place("qp", [P, NG, S], F32R, 4)
    kp = place("kp", [P, 2, 4, S], F32R, 4)
    vp = place("vp", [P, 2, 4 * (P + HD)], F32, 4)
    sc = place("sc", [P, 2, 12 * P], F32, 4)
    pt = place("pt", [P, 2, 12 * P], F32, 4)
    at_t = place("at_t", [P, KT, S], F32, 4)
    rden = place("rden", [P, S], F32, 4)
    assert at[0] <= top, (at[0], top)
    at[0] = xt_at
    xa = place("xa", [P, KT, S], F32, 4)
    assert top <= nc.sbuf_usable_end, (top, nc.sbuf_usable_end)

    ctx = ExitStack()
    with ctx:
        bank = [ctx.enter_context(nc.psum_tensor(f"bank{n}", [P, 512], F32)) for n in range(8)]
        acc = bank[0:4]
        gate_ps, up_ps, z_ps, s_ps = bank[4], bank[5], bank[6], bank[7]

        def sem(name):
            return ctx.enter_context(nc.semaphore(name))

        x_in_s = [sem(f"x_loaded{n}") for n in range(2)]
        tab_in = sem("tables_loaded")
        raw_in = [sem(f"raw_loaded{n}") for n in range(4)]
        aw_in = sem("attn_weights_loaded")
        zeroed = sem("zeroed")
        consts = sem("consts_ready")
        pool_step = sem("pool_step")
        dve_step = sem("dve_step")
        tables = sem("tables_ready")
        dq_raw = sem("raw_unpacked")
        dq_bc = sem("dq_broadcast")
        dq_mul = sem("dq_weight")
        w_hi = sem("w_hi_ready")
        w_lo = sem("w_lo_ready")
        xn_ok = sem("xn_ready")
        tr_ok = sem("xn_transposed")
        xt_hi = sem("xt_hi_ready")
        xt_lo = sem("xt_lo_ready")
        gate_ok = sem("gate_done")
        up_ok = sem("up_done")
        sil_ok = sem("silu_done")
        h_ok = sem("h_done")
        h_hi = sem("h_hi_ready")
        h_lo = sem("h_lo_ready")
        down_ok = sem("down_done")
        x_upd = sem("x_updated")
        spilled = sem("tail_spilled")
        refilled = sem("tail_refilled")
        aw_ok = sem("attn_weights_ready")
        a_xn = sem("attn_xn_ready")
        a_tr = sem("attn_transposed")
        a_xt = sem("attn_xt_ready")
        a_kv = sem("kv_projected")
        a_q = sem("q_projected")
        a_qhi = sem("q_hi_ready")
        a_qlo = sem("q_lo_ready")
        a_kp = sem("k_padded")
        a_vp = sem("v_padded")
        a_s = sem("scores_done")
        a_sb = sem("scores_biased")
        a_max = sem("max_ready")
        a_exp = sem("exp_done")
        a_pt = sem("exp_transposed")
        a_ptc = sem("exp_t_copied")
        a_pv = sem("pv_done")
        a_norm = sem("attn_normed")
        a_y = sem("attn_projected")
        a_x = sem("attn_x_updated")
        stored = sem("out_stored")

        block = ctx.enter_context(nc.Block())

        def w_gu(part, kt, gu, j):
            if j < JA:
                return w_a[:, part, kt, gu, j * P:(j + 1) * P]
            return w_b[:, part, kt, gu, (j - JA) * P:(j - JA) * P + jw(j)]

        def dq_dst(part, c):
            j, kind = divmod(c, 3)
            if kind == 2:
                return w_d[0:jw(j), part, j, :]
            if j < JA:
                return w_a[:, part, 2 * kind:2 * kind + 2, :, j * P:(j + 1) * P]
            return w_b[:, part, 2 * kind:2 * kind + 2, :, (j - JA) * P:(j - JA) * P + jw(j)]

        def chunk_of(buf, c):
            j, kind = divmod(c, 3)
            if kind == 2:
                return buf[0:jw(j), 0:D]
            return buf[:, 0:4 * jw(j)].rearrange("p (k g n) -> p k g n", k=2, g=2)

        NC = 3 * NJ

        @block.sync
        def _(sp):
            for t in range(TT):
                sp.dma_start(x[:, t, :], x_tiles[t]).then_inc(x_in_s[t // 4], 16)
            for c in range(NC):
                j, kind = divmod(c, 3)
                if c >= 4:
                    sp.wait_ge(dq_mul, c - 3)
                if kind == 2:
                    n = jw(j) // 8
                    src = bass.AP(qw_d.tensor, j * (P // 8) * D, [[D, n], [0, 8], [1, D]])
                    sp.dma_start(raw[0:jw(j), c % 4, :], src).then_inc(raw_in[c % 4], 16)
                else:
                    for k in range(2):
                        for g in range(2):
                            row0 = (2 * kind + k) * (P // 8)
                            src = bass.AP(qw_gu.tensor, row0 * 2 * F + g * F + j * P,
                                          [[2 * F, P // 8], [0, 8], [1, jw(j)]])
                            n = (2 * k + g) * jw(j)
                            sp.dma_start(raw[:, c % 4, n:n + jw(j)], src).then_inc(raw_in[c % 4], 16)
            sp.wait_ge(dq_mul, NC)
            sp.wait_ge(w_hi, NC)
            sp.wait_ge(w_lo, NC)
            sp.dma_start(wqkv[:, :, :], w_qkv.rearrange("(k p) n -> p k n", p=P)).then_inc(aw_in, 16)
            sp.dma_start(wo[:, :, :], w_o.rearrange("(k p) n -> p k n", p=P)).then_inc(aw_in, 16)
            tail = w_b[:, :, :, :, :].bitcast(F32).rearrange("p a k g n -> p (a k g n)")
            sp.dma_start(spill, tail).then_inc(spilled, 16)
            sp.wait_ge(spilled, 16)
            sp.wait_ge(a_x, TT)
            sp.dma_start(tail, spill).then_inc(refilled, 16)
            for t in range(TT):
                sp.wait_ge(x_upd, TT + t + 1)
                sp.dma_start(out_tiles[t], x[:, t, :]).then_inc(stored, 16)
            sp.wait_ge(stored, 16 * TT)

        @block.gpsimd
        def _(pool):
            st = Steps(pool, pool_step)
            st.did(nc.gpsimd.iota(pid[:, 0:1], [[0, 1]], base=0, channel_multiplier=1))
            nc.gpsimd.memset(sraw[:, :], 0.0).then_inc(zeroed, 1)
            nc.gpsimd.memset(zraw[:, :], 0).then_inc(zeroed, 1)
            st.did(nc.gpsimd.memset(ident[:, :], 0.0))
            st.did(nc.gpsimd.iota(dist[:, 0, :], [[1, P]], base=0, channel_multiplier=-1,
                                  allow_small_or_imprecise_dtypes=True))
            st.did(nc.gpsimd.iota(dist[:, 1:3, :], [[P, 2], [1, P]], base=-P, channel_multiplier=-1,
                                  allow_small_or_imprecise_dtypes=True))
            st.wait()
            nc.gpsimd.affine_select(out=ident[:, :], in_=ident[:, :], compare_op=ALU.not_equal, fill=1.0,
                                    base=0, pattern=[[-1, P]], channel_multiplier=1).then_inc(consts, 1)
            for n in (0, 2):
                nc.gpsimd.affine_select(out=dist[:, n, :], in_=dist[:, n, :], compare_op=ALU.is_ge,
                                        fill=-1e33, base=0, pattern=[[-1, P]],
                                        channel_multiplier=1).then_inc(consts, 1)
            for c in range(NC):
                pool.wait_ge(w_hi, c + 1)
                nc.gpsimd.tensor_tensor(dq_dst(1, c), chunk_of(wf[:, c % 2, :], c),
                                        dq_dst(0, c).bitcast(F32), ALU.subtract).then_inc(w_lo, 1)

        @block.scalar
        def _(act):
            act.wait_ge(zeroed, 2)
            for r in range(3):
                act.dma_start(sraw[32 * r:32 * r + G_GU, 0:2 * F], sc_gu).then_inc(tab_in, 16)
                act.dma_start(sraw[32 * r:32 * r + G_D, 2 * F:RC], sc_d).then_inc(tab_in, 16)
            act.dma_start(zraw[96:96 + G_GU, 0:F // 4], qz_gu).then_inc(tab_in, 16)
            act.dma_start(zraw[96:96 + G_D, F // 4:RC // 8], qz_d).then_inc(tab_in, 16)
            act.dma_start(gint[:, 0:D], bass.AP(gi_gu.tensor, 0, [[0, P], [1, D]])).then_inc(tab_in, 16)
            act.dma_start(gint[:, D:KC], bass.AP(gi_d.tensor, 0, [[0, P], [1, F]])).then_inc(tab_in, 16)

            def xt_high(s, t):
                n = 4 * s + t
                act.wait_ge(tr_ok, n + 1)
                src = bank[6 + t % 2][:, :].rearrange("p (k n) -> p k n", k=KT)
                nc.scalar.copy(xt[:, 0, :, t * P:(t + 1) * P], src).then_inc(xt_hi, 1)

            def dq_high(c):
                act.wait_ge(dq_mul, c + 1)
                nc.scalar.copy(dq_dst(0, c), chunk_of(wf[:, c % 2, :], c)).then_inc(w_hi, 1)

            def silu(s, j):
                n = NJ * s + j
                act.wait_ge(gate_ok, n + 1)
                if n >= 2:
                    act.wait_ge(h_ok, n - 1)
                nc.scalar.activation(sil[0:jw(j), n % 2, :], gate_ps[0:jw(j), :], ACT.Silu)\
                    .then_inc(sil_ok, 1)

            def h_high(s, j):
                n = NJ * s + j
                act.wait_ge(h_ok, n + 1)
                if n >= 2:
                    act.wait_ge(down_ok, n - 1)
                nc.scalar.copy(hs[0:jw(j), n % 2, 0, :], hf[0:jw(j), n % 2, :]).then_inc(h_hi, 1)

            def ffn(s):
                for j in range(NJ):
                    if s == 0:
                        for c in range(3 * j + 3, min(3 * j + 6, NC)):
                            dq_high(c)
                            if c == 3 * j + 3:
                                silu(s, j)
                        if j == NJ - 1:
                            silu(s, j)
                    else:
                        silu(s, j)
                    h_high(s, j)

            for t in range(4):
                xt_high(0, t)
            for c in range(3):
                dq_high(c)
            ffn(0)
            for t in range(4):
                xt_high(1, t)
            ffn(1)

            with act.Fori(0, B) as b:
                act.wait_ge(a_tr, 2 * b + 1)
                nc.scalar.copy(xa[:, :, 0:P], bank[3][:, :].rearrange("p (k n) -> p k n", k=KT))\
                    .then_inc(a_xt, 1)
                for m in range(KT):
                    act.wait_ge(a_q, KT * b + m + 1)
                    for u in range(2):
                        nc.scalar.activation(qp[0:64, 2 * m + u, :],
                                             bank[m // 2][64 * u:64 * u + 64, (m % 2) * S:(m % 2 + 1) * S],
                                             ACT.Copy, scale=HD ** -0.5).then_inc(a_qhi, 1)

                def exp_t(g):
                    act.wait_ge(a_pt, NG * b + g + 1)
                    if g >= 2:
                        act.wait_ge(a_pv, NG * b + g - 1)
                    for n in range(3):
                        ins = nc.scalar.copy(pt[:, g % 2, 4 * P * n:4 * P * (n + 1)], bank[3 + n][:, :])
                    ins.then_inc(a_ptc, 1)

                for g in range(NG):
                    act.wait_ge(a_max, NG * b + g + 1)
                    for n in range(8):
                        lo, hi = (n * P, n * P + P) if n < 4 else (4 * P + (n - 4) * S, 4 * P + (n - 3) * S)
                        ins = nc.scalar.activation(sc[:, g % 2, lo:hi], sc[:, g % 2, lo:hi], ACT.Exp,
                                                   bias=nmax[:, g % 2, n:n + 1])
                    ins.then_inc(a_exp, 1)
                    if g >= 1:
                        exp_t(g - 1)
                exp_t(NG - 1)

            for s in (2, 3):
                for t in range(4):
                    xt_high(s, t)
                ffn(s)

        @block.vector
        def _(dve):
            st = Steps(dve, dve_step)

            def newton(st, n):
                a, y, u = nwt[:, 1, 0:n], nwt[:, 0, 0:n], nwt[:, 2, 0:n]
                st.wait()
                st.did(nc.vector.tensor_scalar(a, mv[:, 0:n, 1], EPS, None, ALU.add))
                st.wait()
                st.did(nc.vector.tensor_scalar(u.bitcast(I32), a.bitcast(I32), 1, None,
                                               ALU.logical_shift_right))
                st.wait()
                st.did(nc.vector.tensor_scalar(y.bitcast(I32), u.bitcast(I32), -1.0, float(0x5f3759df),
                                               ALU.mult, ALU.add))
                for _ in range(4):
                    st.wait()
                    st.did(nc.vector.tensor_tensor(u, y, y, ALU.mult))
                    st.wait()
                    st.did(nc.vector.tensor_tensor(u, u, a, ALU.mult))
                    st.wait()
                    st.did(nc.vector.tensor_scalar(u, u, -0.5, 1.5, ALU.mult, ALU.add))
                    st.wait()
                    st.did(nc.vector.tensor_tensor(y, y, u, ALU.mult))
                st.wait()

            def moments(st, tile, n):
                st.wait()
                st.did(nc.vector.bn_stats(stats[:, :], tile))
                st.wait()
                nc.vector.memset(nwt[:, 3, 1:2], 0.0)
                st.did(nc.vector.bn_aggr(mv[:, n, :], stats[:, :]))

            def norm_stage(s):
                h = s % 2
                for t in range(4):
                    moments(st, x[:, 4 * h + t, :], t)
                newton(st, 4)

            def xn_tile(s, t):
                n = 4 * s + t
                if t >= 2:
                    dve.wait_ge(tr_ok, n - 1)
                nc.vector.tensor_scalar(xn[:, t % 2, :], x[:, 4 * (s % 2) + t, :], mv[:, t, 0:1],
                                        nwt[:, 0, t:t + 1], ALU.subtract, ALU.mult).then_inc(xn_ok, 1)

            def xt_low(s, t):
                n = 4 * s + t
                dve.wait_ge(xt_hi, n + 1)
                src = bank[6 + t % 2][:, :].rearrange("p (k n) -> p k n", k=KT)
                nc.vector.tensor_tensor(xt[:, 1, :, t * P:(t + 1) * P], src,
                                        xt[:, 0, :, t * P:(t + 1) * P].bitcast(F32), ALU.subtract)\
                    .then_inc(xt_lo, 1)

            def x_transposed(s):
                xn_tile(s, 0)
                xn_tile(s, 1)
                for t in range(4):
                    xt_low(s, t)
                    if t < 2:
                        xn_tile(s, t + 2)

            def dequant(c):
                j, kind = divmod(c, 3)
                dve.wait_ge(raw_in[c % 4], raw_total(c))
                r = chunk_of(raw[:, c % 4, :], c)
                rows = jw(j) if kind == 2 else P
                flat = raw[0:rows, c % 4, 0:(D if kind == 2 else 4 * jw(j))]
                st.did(nc.vector.tensor_scalar(flat, flat, shifts[0:rows, :], 15,
                                               ALU.logical_shift_right, ALU.bitwise_and))
                if c >= 2:
                    dve.wait_ge(w_lo, c - 1)
                dve.wait_ge(dq_bc, c + 1)
                st.wait()
                w = chunk_of(wf[:, c % 2, :], c)
                st.did(nc.vector.tensor_tensor(w, r, chunk_of(z_ps, c), ALU.subtract))
                st.wait()
                nc.vector.tensor_tensor(w, w, chunk_of(s_ps, c), ALU.mult).then_inc(dq_mul, 1)

            def raw_total(c):
                return sum(16 if k % 3 == 2 else 64 for k in range(c % 4, c + 1, 4))

            def h_mul(s, j):
                n = NJ * s + j
                dve.wait_ge(up_ok, n + 1)
                dve.wait_ge(sil_ok, n + 1)
                if n >= 2:
                    dve.wait_ge(h_hi, n - 1)
                nc.vector.tensor_tensor(hf[0:jw(j), n % 2, :], sil[0:jw(j), n % 2, :],
                                        up_ps[0:jw(j), :], ALU.mult).then_inc(h_ok, 1)

            def h_low(s, j):
                n = NJ * s + j
                dve.wait_ge(h_hi, n + 1)
                nc.vector.tensor_tensor(hs[0:jw(j), n % 2, 1, :], hf[0:jw(j), n % 2, :],
                                        hs[0:jw(j), n % 2, 0, :].bitcast(F32), ALU.subtract)\
                    .then_inc(h_lo, 1)

            def ffn(s):
                for j in range(NJ):
                    if s == 0:
                        for c in range(3 * j + 3, min(3 * j + 6, NC)):
                            dequant(c)
                    if s % 2 == 0 and j == NJ - 1:
                        norm_stage(s + 1)
                        xn_tile(s + 1, 0)
                        xn_tile(s + 1, 1)
                    h_mul(s, j)
                    h_low(s, j)
                if s % 2 == 0:
                    for t in range(4):
                        xt_low(s + 1, t)
                        if t < 2:
                            xn_tile(s + 1, t + 2)
                dve.wait_ge(down_ok, NJ * (s + 1))
                for t in range(4):
                    r = x[:, 4 * (s % 2) + t, :]
                    nc.vector.scalar_tensor_tensor(out=r, in0=acc[t][:, :], scalar=0.5, in1=r,
                                                   op0=ALU.mult, op1=ALU.add).then_inc(x_upd, 1)

            dve.wait_ge(pool_step, 1)
            st.did(nc.vector.tensor_scalar(shifts[:, :], pid[:, 0:1], 7, 2, ALU.bitwise_and,
                                           ALU.logical_shift_left))
            st.did(nc.vector.tensor_scalar(pid[:, 1:2], pid[:, 0:1], 31, None, ALU.bitwise_and))
            st.did(nc.vector.tensor_scalar(pid[:, 2:3], pid[:, 0:1], 63, 4, ALU.bitwise_and,
                                           ALU.logical_shift_right))
            st.wait()
            st.did(nc.vector.tensor_copy(row32[:, :], pid[:, 1:2]))
            st.did(nc.vector.tensor_copy(hsel[:, :], pid[:, 2:3]))
            st.wait()
            for h in range(4):
                st.did(nc.vector.tensor_scalar(headmask[:, h:h + 1], hsel[:, :], float(h), None,
                                               ALU.is_equal))
            dve.wait_ge(x_in_s[0], 64)
            norm_stage(0)
            dve.wait_ge(consts, 1)
            x_transposed(0)
            dve.wait_ge(tab_in, 160)
            for rows in (96, 64, 32):
                st.wait()
                st.did(nc.vector.tensor_copy(table[0:rows, :], sraw[0:rows, :]))
                if rows > 32:
                    st.wait()
                    st.did(nc.vector.tensor_tensor(sraw[0:rows - 32, :], sraw[0:rows - 32, :],
                                                   table[0:rows - 32, :], ALU.subtract))
            z = zint[96:128, :].rearrange("p (w e) -> p w e", e=8)
            for e in range(8):
                st.did(nc.vector.tensor_scalar(z[:, :, e], zraw[96:128, :], 4 * e, 15,
                                               ALU.logical_shift_right, ALU.bitwise_and))
            st.wait()
            st.did(nc.vector.tensor_scalar(table[96:128, :], zint[96:128, :], 1.0, None, ALU.add))
            st.wait()
            for lo, hi, n in ((0, D, G_GU), (D, KC, G_D)):
                gi, gf = gint[:, lo:hi], gflt[:, lo:hi]
                st.did(nc.vector.tensor_scalar(gf, gi, 0.0, float(n), ALU.is_lt, ALU.mult))
                st.wait()
                st.did(nc.vector.tensor_tensor(gf, gf, gi, ALU.add))
                st.wait()
                st.did(nc.vector.tensor_scalar(gf, gf, 0.0, float(n - 1), ALU.max, ALU.min))
                st.wait()
                st.did(nc.vector.tensor_scalar(onehot[:, lo:hi], gf, row32[:, :], None, ALU.is_equal))
            st.wait()
            nc.vector.tensor_copy(nwt[:, 3, 0:1], row32[:, :]).then_inc(tables, 1)
            for c in range(3):
                dequant(c)
            dve.wait_ge(x_in_s[1], 64)
            ffn(0)
            ffn(1)

            dve.wait_ge(aw_in, 32)
            k_cols = wqkv[:, :, D:D + HD].unsqueeze(2)
            v_cols = wqkv[:, :, D + HD:D + 2 * HD].unsqueeze(2)
            for k in range(KT):
                for dst, src, n in ((wk8, k_cols, 8), (wv4, v_cols, 4)):
                    nc.vector.tensor_copy(dst[:, k, :].rearrange("p (r n) -> p r n", r=n),
                                          src[:, k].to_broadcast([P, n, HD])).then_inc(aw_ok, 1)
            dve.wait_ge(x_upd, TT)
            dve.wait_ge(spilled, 16)
            st.did(nc.vector.memset(vp[:, :, :], 0.0))
            st.wait()
            strips = vp[:, :, :].rearrange("p k (h n) -> p k h n", n=P + HD)
            st.did(nc.vector.memset(strips[:, :, :, 64:64 + HD], 1.0))

            base, per = st.n, 2 * 2 + 3 + 16
            with dve.Fori(0, B) as b:
                sb = Steps(dve, dve_step, base + per * b)
                for t in range(2):
                    moments(sb, x[:, 2 * b + t, :], t)
                newton(sb, 2)
                for t in range(2):
                    nc.vector.tensor_scalar(xn[:, t, :], x[:, 2 * b + t, :], mv[:, t, 0:1],
                                            nwt[:, 0, t:t + 1], ALU.subtract, ALU.mult).then_inc(a_xn, 1)
                dve.wait_ge(a_tr, 2 * b + 2)
                nc.vector.tensor_copy(xa[:, :, P:S], bank[4][:, :].rearrange("p (k n) -> p k n", k=KT))\
                    .then_inc(a_xt, 1)
                dve.wait_ge(a_kv, b + 1)
                for h in range(4):
                    nc.vector.tensor_scalar(kp[:, 0, h, :], bank[5][:, 0:S], headmask[:, h:h + 1], None,
                                            ALU.mult).then_inc(a_kp, 1)
                for kt in range(2):
                    v4 = bank[5][:, S + kt * 4 * HD:S + (kt + 1) * 4 * HD].rearrange("p (h n) -> p h n", h=4)
                    nc.vector.tensor_copy(strips[:, kt, :, 0:HD], v4).then_inc(a_vp, 1)
                dve.wait_ge(a_kp, 8 * b + 4)
                for h in range(4):
                    nc.vector.scalar_tensor_tensor(out=kp[:, 1, h, :], in0=bank[5][:, 0:S],
                                                   scalar=headmask[:, h:h + 1], in1=kp[:, 0, h, :].bitcast(F32),
                                                   op0=ALU.mult, op1=ALU.subtract).then_inc(a_kp, 1)
                for m in range(KT):
                    for u in range(2):
                        dve.wait_ge(a_qhi, 2 * KT * b + 2 * m + u + 1)
                        nc.vector.scalar_tensor_tensor(
                            out=qp[64:128, 2 * m + u, :],
                            in0=bank[m // 2][64 * u:64 * u + 64, (m % 2) * S:(m % 2 + 1) * S],
                            scalar=HD ** -0.5, in1=qp[0:64, 2 * m + u, :].bitcast(F32),
                            op0=ALU.mult, op1=ALU.subtract).then_inc(a_qlo, 1)

                def normalise(g):
                    o = bank[6 + g % 2]
                    dve.wait_ge(a_pv, NG * b + g + 1)
                    if g >= 1:
                        dve.wait_ge(a_norm, 2 * NG * b + 2 * g)
                    nc.vector.reciprocal(rden[0:64, :], o[64:128, 0:S]).then_inc(a_norm, 1)
                    dve.wait_ge(a_norm, 2 * NG * b + 2 * g + 1)
                    nc.vector.tensor_tensor(at_t[64 * (g % 2):64 * (g % 2) + 64, g // 2, :], o[0:64, 0:S],
                                            rden[0:64, :], ALU.mult).then_inc(a_norm, 1)

                for g in range(NG):
                    dve.wait_ge(a_s, NG * b + g + 1)
                    if g >= 2:
                        dve.wait_ge(a_pt, NG * b + g - 1)
                    for h in range(4):
                        nc.vector.scalar_tensor_tensor(
                            out=sc[:, g % 2, h * P:(h + 1) * P], in0=dist[:, 0, :], scalar=SLOPES[4 * g + h],
                            in1=bank[0][:, h * P:(h + 1) * P], op0=ALU.mult, op1=ALU.add)
                        ins = nc.vector.scalar_tensor_tensor(
                            out=sc[:, g % 2, 4 * P + h * S:4 * P + (h + 1) * S],
                            in0=dist[:, 1:3, :].rearrange("p a b -> p (a b)"), scalar=SLOPES[4 * g + h],
                            in1=bank[1 + h // 2][:, (h % 2) * S:(h % 2 + 1) * S], op0=ALU.mult, op1=ALU.add)
                    ins.then_inc(a_sb, 1)
                    dve.wait_ge(a_sb, NG * b + g + 1)
                    nc.vector.tensor_reduce(nmax[:, g % 2, 0:4],
                                            sc[:, g % 2, 0:4 * P].rearrange("p (h n) -> p h n", h=4),
                                            AX_X, ALU.max, negate=True)
                    nc.vector.tensor_reduce(nmax[:, g % 2, 4:8],
                                            sc[:, g % 2, 4 * P:12 * P].rearrange("p (h n) -> p h n", h=4),
                                            AX_X, ALU.max, negate=True).then_inc(a_max, 1)
                    if g >= 2:
                        normalise(g - 2)
                normalise(NG - 2)
                normalise(NG - 1)
                for t in range(2):
                    dve.wait_ge(a_y, 2 * b + t + 1)
                    nc.vector.tensor_tensor(x[:, 2 * b + t, :], bank[t][:, :], x[:, 2 * b + t, :],
                                            ALU.add).then_inc(a_x, 1)
                assert sb.n == per, (sb.n, per)
            st.n += per * B
            dve.wait_ge(a_x, TT)
            norm_stage(2)
            x_transposed(2)
            ffn(2)
            ffn(3)

        @block.tensor
        def _(pe):
            def transposes(s, t):
                n = 4 * s + t
                pe.wait_ge(xn_ok, n + 1)
                if t >= 2:
                    pe.wait_ge(xt_lo, n - 1)
                for k in range(KT):
                    ins = nc.tensor.transpose(bank[6 + t % 2][:, k * P:(k + 1) * P],
                                              xn[:, t % 2, k * P:(k + 1) * P], ident[:, :])
                ins.then_inc(tr_ok, 1)

            def broadcasts(c):
                j, kind = divmod(c, 3)
                if c >= 1:
                    pe.wait_ge(dq_mul, c)
                for ps, lo, hi in ((z_ps, 96, 128), (s_ps, 0, 96)):
                    if kind == 2:
                        ins = nc.tensor.matmul(ps[0:jw(j), :], onehot[lo:hi, D + j * P:D + j * P + jw(j)],
                                               table[lo:hi, 2 * F:RC], start=True, stop=True)
                    else:
                        cols = table[lo:hi, 0:2 * F].rearrange("p (g n) -> p g n", g=2)[:, :, j * P:j * P + jw(j)]
                        for k in range(2):
                            kt = 2 * kind + k
                            ins = nc.tensor.matmul(
                                ps[:, 2 * k * jw(j):2 * (k + 1) * jw(j)].rearrange("p (g n) -> p g n", g=2),
                                onehot[lo:hi, kt * P:(kt + 1) * P], cols, start=True, stop=True)
                ins.then_inc(dq_bc, 1)

            PARTS = ((0, 0), (1, 0), (0, 1))

            def gate_up(s, j, gu):
                n = NJ * s + j
                if j == 0 and gu == 0:
                    pe.wait_ge(xt_hi, 4 * (s + 1))
                    pe.wait_ge(xt_lo, 4 * (s + 1))
                if s == 0 and gu == 0:
                    pe.wait_ge(w_hi, 3 * j + 2)
                    pe.wait_ge(w_lo, 3 * j + 2)
                if s == 2 and j == JA and gu == 0:
                    pe.wait_ge(refilled, 16)
                if n >= 1:
                    pe.wait_ge(*((sil_ok, n) if gu == 0 else (h_ok, n)))
                ps = (gate_ps, up_ps)[gu]
                for k in range(KT):
                    for q, (a, b) in enumerate(PARTS):
                        ins = nc.tensor.matmul(ps[0:jw(j), :], w_gu(a, k, gu, j), xt[:, b, k, :],
                                               start=(k == 0 and q == 0), stop=(k == KT - 1 and q == 2))
                ins.then_inc((gate_ok, up_ok)[gu], 1)

            def down(s, j):
                n = NJ * s + j
                pe.wait_ge(h_hi, n + 1)
                pe.wait_ge(h_lo, n + 1)
                if s == 0:
                    pe.wait_ge(w_hi, 3 * j + 3)
                    pe.wait_ge(w_lo, 3 * j + 3)
                if s in (1, 3) and j == 0:
                    pe.wait_ge(x_upd, 4 * s)
                for t in range(4):
                    for q, (a, b) in enumerate(PARTS):
                        ins = nc.tensor.matmul(acc[t][:, :], hs[0:jw(j), n % 2, a, t * P:(t + 1) * P],
                                               w_d[0:jw(j), b, j, :],
                                               start=(j == 0 and q == 0), stop=(j == NJ - 1 and q == 2))
                ins.then_inc(down_ok, 1)

            def ffn(s):
                for j in range(NJ):
                    gate_up(s, j, 0)
                    if s == 0 and j + 1 < NJ:
                        broadcasts(3 * j + 3)
                    gate_up(s, j, 1)
                    if s == 0 and j + 1 < NJ:
                        broadcasts(3 * j + 4)
                    if j >= 1:
                        if j == NJ - 1 and s % 2 == 0:
                            transposes(s + 1, 0)
                            transposes(s + 1, 1)
                        down(s, j - 1)
                    if s == 0 and j + 1 < NJ:
                        broadcasts(3 * j + 5)
                if s % 2 == 0:
                    transposes(s + 1, 2)
                    transposes(s + 1, 3)
                down(s, NJ - 1)

            pe.wait_ge(consts, 1)
            for t in range(4):
                transposes(0, t)
            pe.wait_ge(tables, 1)
            pe.wait_ge(xt_lo, 4)
            for c in range(3):
                broadcasts(c)
            ffn(0)
            ffn(1)

            pe.wait_ge(aw_ok, 2 * KT)
            pe.wait_ge(consts, 3)
            with pe.Fori(0, B) as b:
                for t in range(2):
                    pe.wait_ge(a_xn, 2 * b + t + 1)
                    for k in range(KT):
                        ins = nc.tensor.transpose(bank[3 + t][:, k * P:(k + 1) * P],
                                                  xn[:, t, k * P:(k + 1) * P], ident[:, :])
                    ins.then_inc(a_tr, 1)
                pe.wait_ge(a_xt, 2 * b + 2)
                for k in range(KT):
                    nc.tensor.matmul(bank[5][:, 0:S], wk8[:, k, :], xa[:, k, :], start=(k == 0),
                                     stop=(k == KT - 1))
                for kt in range(2):
                    for k in range(KT):
                        ins = nc.tensor.matmul(bank[5][:, S + kt * 4 * HD:S + (kt + 1) * 4 * HD],
                                               xa[:, k, kt * P:(kt + 1) * P], wv4[:, k, :],
                                               start=(k == 0), stop=(k == KT - 1))
                ins.then_inc(a_kv, 1)
                for m in range(KT):
                    if m % 2:
                        pe.wait_ge(a_qlo, 2 * KT * b + 2 * m)
                    for k in range(KT):
                        ins = nc.tensor.matmul(bank[m // 2][:, (m % 2) * S:(m % 2 + 1) * S],
                                               wqkv[:, k, m * P:(m + 1) * P], xa[:, k, :],
                                               start=(k == 0), stop=(k == KT - 1))
                    ins.then_inc(a_q, 1)

                def scores(g):
                    if g == 0:
                        pe.wait_ge(a_qlo, 2 * KT * b + 2 * KT)
                        pe.wait_ge(a_kp, 8 * b + 8)
                    else:
                        pe.wait_ge(a_sb, NG * b + g)
                    for part in range(2):
                        nc.tensor.matmul(bank[0][:, :].rearrange("p (h n) -> p h n", h=4),
                                         qp[:, g, 0:P], kp[:, part, :, 0:P], start=(part == 0),
                                         stop=(part == 1))
                    for u in range(2):
                        for part in range(2):
                            ins = nc.tensor.matmul(bank[1 + u][:, :].rearrange("p (h n) -> p h n", h=2),
                                                   qp[:, g, P:S], kp[:, part, 2 * u:2 * u + 2, :],
                                                   start=(part == 0), stop=(part == 1))
                    ins.then_inc(a_s, 1)

                def exp_transposes(g):
                    pe.wait_ge(a_exp, NG * b + g + 1)
                    if g >= 1:
                        pe.wait_ge(a_ptc, NG * b + g)
                    for h in range(4):
                        lo = h * P
                        hi = 4 * P + h * S
                        keys0 = bank[3 + h // 2][:, (h % 2) * S:(h % 2 + 1) * S]
                        nc.tensor.transpose(keys0[:, 0:P], sc[:, g % 2, lo:lo + P], ident[:, :])
                        nc.tensor.transpose(keys0[:, P:S], sc[:, g % 2, hi:hi + P], ident[:, :])
                        ins = nc.tensor.transpose(bank[5][:, h * P:(h + 1) * P],
                                                  sc[:, g % 2, hi + P:hi + S], ident[:, :])
                    ins.then_inc(a_pt, 1)

                def weighted_values(g):
                    pe.wait_ge(a_ptc, NG * b + g + 1)
                    if g == 0:
                        pe.wait_ge(a_vp, 2 * b + 2)
                    if g >= 2:
                        pe.wait_ge(a_norm, 2 * NG * b + 2 * (g - 1))
                    o = bank[6 + g % 2]
                    for h in range(4):
                        nc.tensor.matmul(o[:, 0:S], vp[:, 0, h * P:(h + 1) * P],
                                         pt[:, g % 2, h * S:(h + 1) * S], start=(h == 0), stop=False,
                                         skip_group_check=True)
                        ins = nc.tensor.matmul(o[:, P:S], vp[:, 1, h * P:(h + 1) * P],
                                               pt[:, g % 2, 8 * P + h * P:8 * P + (h + 1) * P],
                                               start=False, stop=(h == 3), skip_group_check=True)
                    ins.then_inc(a_pv, 1)

                scores(0)
                for g in range(NG):
                    if g + 1 < NG:
                        scores(g + 1)
                    exp_transposes(g)
                    if g >= 1:
                        weighted_values(g - 1)
                weighted_values(NG - 1)
                pe.wait_ge(a_norm, 2 * NG * b + 2 * NG)
                for t in range(2):
                    for k in range(KT):
                        ins = nc.tensor.matmul(bank[t][:, :], at_t[:, k, t * P:(t + 1) * P], wo[:, k, :],
                                               start=(k == 0), stop=(k == KT - 1))
                    ins.then_inc(a_y, 1)

            for t in range(4):
                transposes(2, t)
            ffn(2)
            ffn(3)


_INS = ["L0_attn_hidden_states", "L0_attn_Wqkv", "L0_attn_Wo", "L0_ffn_qweight_gu", "L0_ffn_qzeros_gu",
        "L0_ffn_scales_gu", "L0_ffn_g_idx_gu", "L0_ffn_qweight_down", "L0_ffn_qzeros_down",
        "L0_ffn_scales_down", "L0_ffn_g_idx_down"]


def kernel(**inputs):
    import concourse.bacc as bacc
    from concourse.bass_utils import run_bass_kernel_spmd

    nc = bacc.Bacc("TRN2", target_bir_lowering=False, num_devices=1)
    arrays, args = {}, []
    for name in _INS:
        a = np.ascontiguousarray(inputs[name])
        if a.dtype == np.uint32:
            a = a.view(np.int32)
        arrays[f"in_{name}"] = a
        args.append(nc.dram_tensor(f"in_{name}", a.shape, mybir.dt.from_np(a.dtype), kind="ExternalInput").ap())
    shape = inputs["L0_attn_hidden_states"].shape
    out = nc.dram_tensor("out", shape, F32, kind="ExternalOutput").ap()
    macaron_block(nc, *args, out)
    r = run_bass_kernel_spmd(nc, [arrays], core_ids=[0])
    return r.results[0]["out"]
```

```python
from contextlib import ExitStack

import numpy as np

import concourse.bass as bass
from concourse import mybir

F32 = mybir.dt.float32
F32R = mybir.dt.float32r
BF16 = mybir.dt.bfloat16
I32 = mybir.dt.int32
U32 = mybir.dt.uint32
ALU = mybir.AluOpType
ACT = mybir.ActivationFunctionType
AX_X = mybir.AxisListType.X

P = 128
EPS = 1e-5


def alibi_slopes(n):
    cp2 = 2 ** int(np.floor(np.log2(n)))
    base = 2.0 ** (-2.0 ** (-(np.log2(cp2) - 3)))
    return [float(np.float32(v)) for v in base ** np.arange(1, n + 1, dtype=np.float64)]


class Steps:

    def __init__(self, eng, sem, base=0):
        self.eng, self.sem, self.base, self.n = eng, sem, base, 0

    def did(self, ins):
        ins.then_inc(self.sem, 1)
        self.n += 1

    def wait(self):
        self.eng.wait_ge(self.sem, self.base + self.n)


def macaron_block(nc, x_in, w_qkv, w_o, qw_gu, qz_gu, sc_gu, gi_gu, qw_d, qz_d, sc_d, gi_d, out):
    B, S, D = x_in.shape
    T = B * S
    HD = (w_qkv.shape[1] - D) // 2
    NH = D // HD
    F = qw_d.shape[0] * 8
    G_GU, G_D = sc_gu.shape[0], sc_d.shape[0]
    TT = T // P
    KT = D // P
    NJ = (F + P - 1) // P
    HALF = 4 * P
    NHALF = T // HALF
    JA = 3
    FA, FB = JA * P, F - JA * P
    NG = NH // 4
    SLOPES = alibi_slopes(NH)
    RC = 2 * F + D
    KC = D + F
    EARLY = 2 * P
    assert (D, HD, S, TT % 4, NHALF) == (512, 16, 2 * P, 0, 2)

    def jw(j):
        return min(P, F - j * P)

    x_tiles = x_in.rearrange("b (t p) d -> (b t) p d", p=P)
    out_tiles = out.rearrange("b (t p) d -> (b t) p d", p=P)
    spill = nc.dram_tensor("gate_up_tail", (P, 2 * KT * 2 * FB), F32, kind="Internal").ap()

    at = [(nc.sbuf_base + 31) // 32 * 32]

    def place(name, shape, dt, size):
        t = nc.alloc_sbuf_tensor_at(name, shape, dt, offset=at[0])
        n = int(np.prod(shape[1:])) * size
        at[0] += (n + 31) // 32 * 32
        return t

    x = place("x", [P, TT, D], F32, 4)
    w_a = place("w_a", [P, 2, KT, 2, FA], F32R, 4)
    w_d = place("w_d", [P, 2, NJ, D], F32R, 4)
    xt_at = at[0]
    xt = place("xt", [P, 2, KT, HALF], F32R, 4)
    xn = place("xn", [P, 2, D], F32, 4)
    ident = place("ident", [P, P], F32, 4)
    dist = place("dist", [P, 3, P], F32, 4)
    pid = place("pid", [P, 4], I32, 4)
    shifts = place("shifts", [P, 1], I32, 4)
    row32 = place("row32", [P, 1], F32, 4)
    headmask = place("headmask", [P, 4], F32, 4)
    hsel = place("hsel", [P, 1], F32, 4)
    stats = place("stats", [P, 4, 6], F32, 4)
    mv = place("mv", [P, TT, 2], F32, 4)
    rstd = place("rstd", [P, TT], F32, 4)
    nwt = place("nwt", [P, 2, 4], F32, 4)
    nmax = place("nmax", [P, 4, 4], F32, 4)
    dq_at = at[0]
    table = place("table", [P, RC], BF16, 2)
    onehot = place("onehot", [P, KC], BF16, 2)
    raw = place("raw", [P, 4, 512], I32, 4)
    wf = place("wf", [P, 2, 512], F32, 4)
    ff_at = at[0] = max(at[0], dq_at + 4 * (KT * (D + 9 * HD) + KT * D + KT * S))
    sil = place("sil", [P, 2, HALF], F32, 4)
    hf = place("hf", [P, 2, HALF], F32, 4)
    hs = place("hs", [P, 2, 2, HALF], F32R, 4)
    tail_at = at[0]
    w_b = place("w_b", [P, 2, KT, 2, FB], F32R, 4)
    top = at[0]
    at[0] = tail_at
    sraw = place("sraw", [P, RC], F32, 4)
    zint = place("zint", [P, RC], I32, 4)
    zraw = place("zraw", [P, RC // 8], I32, 4)
    gint = place("gint", [P, KC], I32, 4)
    gflt = place("gflt", [P, KC], F32, 4)
    assert at[0] <= top
    at[0] = dq_at
    wqkv = place("wqkv", [P, KT, D + 9 * HD], F32, 4)
    wo = place("wo", [P, KT, D], F32, 4)
    xa = place("xa", [P, KT, S], F32, 4)
    assert at[0] <= ff_at
    at[0] = ff_at
    sc = place("sc", [P, 4, 4 * P], F32, 4)
    at_t = place("at_t", [P, 2, KT, S], F32, 4)
    assert at[0] <= tail_at
    qp = place("qp", [P, 2, NG, S], F32R, 4)
    kp = place("kp", [P, 2, 2, 4, S], F32R, 4)
    vp = place("vp", [P, 2, 2, 4 * (P + HD)], F32, 4)
    pt = place("pt", [P, 2, 12 * P], F32, 4)
    rden = place("rden", [P, S], F32, 4)
    assert at[0] <= top, (at[0], top)
    assert top <= nc.sbuf_usable_end, (top, nc.sbuf_usable_end)

    ctx = ExitStack()
    with ctx:
        bank = [ctx.enter_context(nc.psum_tensor(f"bank{n}", [P, 512], F32)) for n in range(8)]
        acc = bank[0:4]
        gate_ps, up_ps, z_ps, s_ps = bank[4], bank[5], bank[6], bank[7]

        def sem(name):
            return ctx.enter_context(nc.semaphore(name))

        x_in_s = [sem(f"x_loaded{n}") for n in range(5)]
        z_in = sem("zeros_loaded")
        gi_in = sem("groups_loaded")
        sa_in = sem("scales_early_loaded")
        sb_in = sem("scales_rest_loaded")
        raw_in = [sem(f"raw_loaded{n}") for n in range(4)]
        aw_in = sem("attn_weights_loaded")
        zeroed = sem("load_buffers_zeroed")
        zeroed_a = sem("early_scales_zeroed")
        consts = sem("consts_ready")
        rows_ok = sem("row_numbers_ready")
        pool_step = sem("pool_step")
        dve_step = sem("dve_step")
        z_unpacked = sem("zeros_unpacked")
        z_tab = sem("zeros_in_table")
        s_early = sem("early_scales_in_table")
        s_conv = sem("scale_part_converted")
        s_sub = sem("scale_rest_computed")
        oh_gu = sem("onehot_gate_up_ready")
        oh_d = sem("onehot_down_ready")
        dq_bc = sem("dq_broadcast")
        dq_mul = sem("dq_weight")
        w_hi = sem("w_hi_ready")
        w_lo = sem("w_lo_ready")
        spilled = sem("tail_spilled")
        refilled = sem("tail_refilled")
        xn_ok = sem("xn_ready")
        tr_ok = sem("xn_transposed")
        xt_hi = sem("xt_hi_ready")
        xt_lo = sem("xt_lo_ready")
        gate_ok = sem("gate_done")
        up_ok = sem("up_done")
        sil_ok = sem("silu_done")
        h_ok = sem("h_done")
        h_hi = sem("h_hi_ready")
        h_lo = sem("h_lo_ready")
        down_ok = sem("down_done")
        x_upd = sem("x_updated")
        vp_set = sem("v_blocks_set")
        a_xt = sem("attn_xt_ready")
        a_kv = sem("kv_projected")
        a_q = sem("q_projected")
        a_qhi = sem("q_hi_ready")
        a_qlo = sem("q_lo_ready")
        a_khi = sem("k_hi_padded")
        a_klo = sem("k_lo_padded")
        a_vp = sem("v_padded")
        a_s = sem("scores_done")
        a_sb = sem("scores_biased")
        a_max = sem("max_ready")
        a_exp = sem("exp_done")
        a_pt = sem("exp_transposed")
        a_ptc = sem("exp_t_copied")
        a_pv = sem("pv_done")
        a_norm = sem("attn_normed")
        a_y = sem("attn_projected")
        a_x = sem("attn_x_updated")
        stored = sem("out_stored")

        block = ctx.enter_context(nc.Block())

        NC = 3 * NJ
        LAST = NG * B - 1
        early_gu = slice(0, EARLY)
        strips = vp[:, :, :, :].rearrange("p b k (h n) -> p b k h n", n=P + HD)

        def tile_no(kind, s, t):
            return {"ffn": 4 * s + t + (8 if s >= 2 else 0), "attn": 8 + 2 * s + t}[kind]

        def w_gu(part, kt, gu, j):
            if j < JA:
                return w_a[:, part, kt, gu, j * P:(j + 1) * P]
            return w_b[:, part, kt, gu, (j - JA) * P:(j - JA) * P + jw(j)]

        def dq_dst(part, c):
            j, kind = divmod(c, 3)
            if kind == 2:
                return w_d[0:jw(j), part, j, :]
            if j < JA:
                return w_a[:, part, 2 * kind:2 * kind + 2, :, j * P:(j + 1) * P]
            return w_b[:, part, 2 * kind:2 * kind + 2, :, (j - JA) * P:(j - JA) * P + jw(j)]

        def chunk_of(buf, c):
            j, kind = divmod(c, 3)
            if kind == 2:
                return buf[0:jw(j), 0:D]
            return buf[:, 0:4 * jw(j)].rearrange("p (k g n) -> p k g n", k=2, g=2)

        def gu_cols(t, cols):
            return t[:, 0:2 * F].rearrange("p (g n) -> p g n", g=2)[:, :, cols]

        @block.sync
        def _(sp):
            def load_raw(c):
                j, kind = divmod(c, 3)
                if c >= 4:
                    sp.wait_ge(dq_mul, c - 3)
                if kind == 2:
                    src = bass.AP(qw_d.tensor, j * (P // 8) * D, [[D, jw(j) // 8], [0, 8], [1, D]])
                    sp.dma_start(raw[0:jw(j), c % 4, :], src).then_inc(raw_in[c % 4], 16)
                    return
                for k in range(2):
                    for g in range(2):
                        row0 = (2 * kind + k) * (P // 8)
                        src = bass.AP(qw_gu.tensor, row0 * 2 * F + g * F + j * P,
                                      [[2 * F, P // 8], [0, 8], [1, jw(j)]])
                        n = (2 * k + g) * jw(j)
                        sp.dma_start(raw[:, c % 4, n:n + jw(j)], src).then_inc(raw_in[c % 4], 16)

            for t in range(4):
                sp.dma_start(x[:, t, :], x_tiles[t]).then_inc(x_in_s[t], 16)
            sp.dma_start(gint[:, D:KC], bass.AP(gi_d.tensor, 0, [[0, P], [1, F]])).then_inc(gi_in, 16)
            for c in range(3):
                load_raw(c)
            for t in range(4, TT):
                sp.dma_start(x[:, t, :], x_tiles[t]).then_inc(x_in_s[4], 16)
            for c in range(3, NC):
                load_raw(c)
            sp.wait_ge(w_lo, NC)
            qkv_rows = w_qkv.rearrange("(k p) n -> p k n", p=P)
            sp.dma_start(wqkv[:, :, 0:D], qkv_rows[:, :, 0:D]).then_inc(aw_in, 16)
            sp.dma_start(wqkv[:, :, D + 8 * HD:D + 9 * HD], qkv_rows[:, :, D + HD:D + 2 * HD])\
                .then_inc(aw_in, 16)
            for k in range(KT):
                src = qkv_rows[:, k, D:D + HD].unsqueeze(1).to_broadcast([P, 8, HD])
                sp.dma_start(wqkv[:, k, D:D + 8 * HD].rearrange("p (c n) -> p c n", c=8), src)\
                    .then_inc(aw_in, 16)
            sp.dma_start(wo[:, :, :], w_o.rearrange("(k p) n -> p k n", p=P)).then_inc(aw_in, 16)
            tail = w_b[:, :, :, :, :].bitcast(F32).rearrange("p a k g n -> p (a k g n)")
            sp.dma_start(spill, tail).then_inc(spilled, 16)
            sp.wait_ge(spilled, 16)
            sp.wait_ge(a_pv, LAST + 1)
            sp.wait_ge(a_norm, 2 * (LAST + 1))
            sp.dma_start(tail, spill).then_inc(refilled, 16)
            sp.wait_ge(refilled, 16)
            for t in range(TT):
                sp.wait_ge(x_upd, TT + t + 1)
                sp.dma_start(out_tiles[t], x[:, t, :]).then_inc(stored, 16)
            sp.wait_ge(stored, 16 * TT)

        @block.gpsimd
        def _(pool):
            st = Steps(pool, pool_step)
            st.did(nc.gpsimd.iota(pid[:, 0:1], [[0, 1]], base=0, channel_multiplier=1))
            nc.gpsimd.memset(zraw[:, :], 0).then_inc(zeroed, 1)
            nc.gpsimd.memset(gu_cols(sraw, slice(EARLY, F)), 0.0).then_inc(zeroed, 1)
            st.did(nc.gpsimd.memset(ident[:, :], 0.0))
            st.did(nc.gpsimd.iota(dist[:, 0, :], [[1, P]], base=0, channel_multiplier=-1,
                                  allow_small_or_imprecise_dtypes=True))
            st.did(nc.gpsimd.iota(dist[:, 1:3, :], [[P, 2], [1, P]], base=-P, channel_multiplier=-1,
                                  allow_small_or_imprecise_dtypes=True))
            st.wait()
            nc.gpsimd.affine_select(out=ident[:, :], in_=ident[:, :], compare_op=ALU.not_equal, fill=1.0,
                                    base=0, pattern=[[-1, P]], channel_multiplier=1).then_inc(consts, 1)
            for n in (0, 2):
                nc.gpsimd.affine_select(out=dist[:, n, :], in_=dist[:, n, :], compare_op=ALU.is_ge,
                                        fill=-1e33, base=0, pattern=[[-1, P]],
                                        channel_multiplier=1).then_inc(consts, 1)
            pool.wait_ge(gi_in, 32)
            pool.wait_ge(rows_ok, 1)
            gi, gf = gint[:, D:KC], gflt[:, D:KC]
            st.did(nc.gpsimd.tensor_scalar(gf.bitcast(I32), gi, 0.0, float(G_D), ALU.is_lt, ALU.mult))
            st.wait()
            st.did(nc.gpsimd.tensor_tensor(gi, gf.bitcast(I32), gi, ALU.add))
            st.wait()
            st.did(nc.gpsimd.tensor_scalar(gf, gi, float(G_D - 1), 0.0, ALU.min, ALU.max))
            st.wait()
            nc.gpsimd.tensor_scalar(onehot[:, D:KC], gf, row32[:, :], None, ALU.is_equal).then_inc(oh_d, 1)
            for c in range(NC):
                pool.wait_ge(w_hi, c + 1)
                nc.gpsimd.tensor_tensor(dq_dst(1, c), chunk_of(wf[:, c % 2, :], c),
                                        dq_dst(0, c).bitcast(F32), ALU.subtract).then_inc(w_lo, 1)
            pool.wait_ge(spilled, 16)
            pool.wait_ge(up_ok, 2 * NJ)
            st.did(nc.gpsimd.memset(vp[:, :, :, :], 0.0))
            st.wait()
            for b in range(2):
                nc.gpsimd.memset(strips[:, b, :, :, 64:64 + HD], 1.0).then_inc(vp_set, 1)

        @block.scalar
        def _(act):
            act.dma_start(gint[:, 0:D], bass.AP(gi_gu.tensor, 0, [[0, P], [1, D]])).then_inc(gi_in, 16)
            act.wait_ge(zeroed, 1)
            act.dma_start(zraw[96:96 + G_GU, 0:F // 4], qz_gu).then_inc(z_in, 16)
            act.dma_start(zraw[96:96 + G_D, F // 4:RC // 8], qz_d).then_inc(z_in, 16)
            act.wait_ge(zeroed_a, 2)
            gu3 = sc_gu.rearrange("r (g n) -> r g n", g=2)
            for r in range(3):
                act.dma_start(gu_cols(sraw[32 * r:32 * r + G_GU, :], early_gu), gu3[:, :, early_gu])\
                    .then_inc(sa_in, 16)
                act.dma_start(sraw[32 * r:32 * r + G_D, 2 * F:RC], sc_d).then_inc(sa_in, 16)
            act.wait_ge(zeroed, 2)
            for r in range(3):
                act.dma_start(gu_cols(sraw[32 * r:32 * r + G_GU, :], slice(EARLY, F)),
                              gu3[:, :, EARLY:F]).then_inc(sb_in, 16)
            act.wait_ge(z_unpacked, 8)
            nc.scalar.copy(gu_cols(table[96:128, :], early_gu), gu_cols(zint[96:128, :], early_gu))\
                .then_inc(z_tab, 1)
            nc.scalar.copy(table[96:128, 2 * F:RC], zint[96:128, 2 * F:RC]).then_inc(z_tab, 1)

            def xt_high(s, t):
                act.wait_ge(tr_ok, tile_no("ffn", s, t) + 1)
                src = bank[6 + t % 2][:, :].rearrange("p (k n) -> p k n", k=KT)
                nc.scalar.copy(xt[:, 0, :, t * P:(t + 1) * P], src).then_inc(xt_hi, 1)

            def dq_high(c):
                act.wait_ge(dq_mul, c + 1)
                nc.scalar.copy(dq_dst(0, c), chunk_of(wf[:, c % 2, :], c)).then_inc(w_hi, 1)

            def silu(s, j):
                n = NJ * s + j
                act.wait_ge(gate_ok, n + 1)
                if n >= 2:
                    act.wait_ge(h_ok, n - 1)
                nc.scalar.activation(sil[0:jw(j), n % 2, :], gate_ps[0:jw(j), :], ACT.Silu)\
                    .then_inc(sil_ok, 1)

            def h_high(s, j):
                n = NJ * s + j
                act.wait_ge(h_ok, n + 1)
                if n >= 2:
                    act.wait_ge(down_ok, n - 1)
                nc.scalar.copy(hs[0:jw(j), n % 2, 0, :], hf[0:jw(j), n % 2, :]).then_inc(h_hi, 1)

            def x_copy(b):
                for t in range(2):
                    act.wait_ge(tr_ok, tile_no("attn", b, t) + 1)
                    nc.scalar.copy(xa[:, :, t * P:(t + 1) * P],
                                   bank[6 + t][:, :].rearrange("p (k n) -> p k n", k=KT)).then_inc(a_xt, 1)

            def k_high(b):
                act.wait_ge(a_kv, b + 1)
                for h in range(4):
                    nc.scalar.activation(kp[:, b % 2, 0, h, :], bank[6][:, 0:S], ACT.Copy,
                                         scale=headmask[:, h:h + 1]).then_inc(a_khi, 1)

            def q_high(b, i):
                act.wait_ge(a_q, 2 * b + i + 1)
                for g in range(4 * i, 4 * i + 4):
                    src = bank[7 - i][64 * (g % 2):64 * (g % 2) + 64, (g // 2 % 2) * S:(g // 2 % 2 + 1) * S]
                    nc.scalar.activation(qp[0:64, b % 2, g, :], src, ACT.Copy, scale=HD ** -0.5)\
                        .then_inc(a_qhi, 1)

            def scale_rest(r):
                rows = 96 - 32 * r
                if r == 0:
                    act.wait_ge(sb_in, 48)
                else:
                    act.wait_ge(s_sub, r)
                nc.scalar.copy(gu_cols(table[0:rows, :], slice(EARLY, F)),
                               gu_cols(sraw[0:rows, :], slice(EARLY, F))).then_inc(s_conv, 1)

            for t in range(4):
                xt_high(0, t)
            nc.scalar.copy(gu_cols(table[96:128, :], slice(EARLY, F)),
                           gu_cols(zint[96:128, :], slice(EARLY, F))).then_inc(z_tab, 1)
            for c in range(3):
                dq_high(c)
                scale_rest(c)
            for j in range(NJ):
                if j + 1 < NJ:
                    dq_high(3 * j + 3)
                silu(0, j)
                if j + 1 < NJ:
                    dq_high(3 * j + 4)
                h_high(0, j)
                if j + 1 < NJ:
                    dq_high(3 * j + 5)
            for t in range(4):
                xt_high(1, t)
            for j in range(NJ):
                silu(1, j)
                h_high(1, j)
                if j == 6:
                    act.wait_ge(w_lo, NC)
                    x_copy(0)
            act.wait_ge(spilled, 16)
            k_high(0)
            q_high(0, 0)
            q_high(0, 1)

            def exps(n):
                act.wait_ge(a_max, n + 1)
                heads, w = (4, P) if n % 3 == 0 else (2, S)
                for h in range(heads):
                    r = sc[:, n % 4, h * w:(h + 1) * w]
                    ins = nc.scalar.activation(r, r, ACT.Exp, bias=nmax[:, n % 4, h:h + 1])
                ins.then_inc(a_exp, 1)

            def exp_t(n):
                g, u = divmod(n, 3)
                act.wait_ge(a_pt, n + 1)
                heads = pt[:, g % 2, :].rearrange("p (h n) -> p h n", h=4)
                if u == 0:
                    dst, src = heads[:, :, 0:P], bank[2 + n % 2][:, :].rearrange("p (h n) -> p h n", h=4)
                else:
                    dst = heads[:, 2 * u - 2:2 * u, P:3 * P]
                    src = bank[2 + n % 2][:, :].rearrange("p (h n) -> p h n", h=2)
                nc.scalar.copy(dst, src).then_inc(a_ptc, 1)

            def between(m):
                b, g = divmod(m, NG)
                if b + 1 < B:
                    if g == 4:
                        x_copy(b + 1)
                    if g == 5:
                        k_high(b + 1)
                    if g in (6, 7):
                        q_high(b + 1, g - 6)
                elif g in (4, 6):
                    xt_high(2, g - 4)
                    xt_high(2, g - 3)

            for n in range(3):
                exps(n)
            for m in range(LAST + 1):
                for u in range(3):
                    if m < LAST:
                        exps(3 * m + 3 + u)
                    exp_t(3 * m + u)
                    if u == 0:
                        between(m)

            for j in range(NJ):
                silu(2, j)
                h_high(2, j)
            for t in range(4):
                xt_high(3, t)
            for j in range(NJ):
                silu(3, j)
                h_high(3, j)

        @block.vector
        def _(dve):
            st = Steps(dve, dve_step)

            def moments(tiles):
                for t in tiles:
                    st.did(nc.vector.bn_stats(stats[:, t % 4, :], x[:, t, :]))
                st.wait()
                for t in tiles:
                    st.did(nc.vector.bn_aggr(mv[:, t, :], stats[:, t % 4, :]))

            def rstds(half):
                a, u, y = nwt[:, 0, :], nwt[:, 1, :], rstd[:, 4 * half:4 * half + 4]
                st.wait()
                st.did(nc.vector.tensor_scalar(a, mv[:, 4 * half:4 * half + 4, 1], EPS, None, ALU.add))
                st.wait()
                st.did(nc.vector.tensor_scalar(u.bitcast(I32), a.bitcast(I32), 1, None,
                                               ALU.logical_shift_right))
                st.wait()
                st.did(nc.vector.tensor_scalar(y.bitcast(I32), u.bitcast(I32), -1.0, float(0x5f3759df),
                                               ALU.mult, ALU.add))
                for _ in range(3):
                    st.wait()
                    st.did(nc.vector.tensor_tensor(u, y, y, ALU.mult))
                    st.wait()
                    st.did(nc.vector.tensor_tensor(u, u, a, ALU.mult))
                    st.wait()
                    st.did(nc.vector.tensor_scalar(u, u, -0.5, 1.5, ALU.mult, ALU.add))
                    st.wait()
                    st.did(nc.vector.tensor_tensor(y, y, u, ALU.mult))
                st.wait()

            def xn_tile(n, tile):
                if n >= 2:
                    dve.wait_ge(tr_ok, n - 1)
                nc.vector.tensor_scalar(xn[:, n % 2, :], x[:, tile, :], mv[:, tile, 0:1],
                                        rstd[:, tile:tile + 1], ALU.subtract, ALU.mult).then_inc(xn_ok, 1)

            def xt_low(s, t):
                dve.wait_ge(xt_hi, 4 * s + t + 1)
                src = bank[6 + t % 2][:, :].rearrange("p (k n) -> p k n", k=KT)
                nc.vector.tensor_tensor(xt[:, 1, :, t * P:(t + 1) * P], src,
                                        xt[:, 0, :, t * P:(t + 1) * P].bitcast(F32), ALU.subtract)\
                    .then_inc(xt_lo, 1)

            def ffn_xn(s, t):
                xn_tile(tile_no("ffn", s, t), 4 * (s % 2) + t)

            def dequant(c):
                kind = c % 3
                dve.wait_ge(raw_in[c % 4], sum(16 if k % 3 == 2 else 64 for k in range(c % 4, c + 1, 4)))
                rows = jw(c // 3) if kind == 2 else P
                flat = raw[0:rows, c % 4, 0:(D if kind == 2 else 4 * jw(c // 3))]
                st.did(nc.vector.tensor_scalar(flat, flat, shifts[0:rows, :], 15,
                                               ALU.logical_shift_right, ALU.bitwise_and))
                if c >= 2:
                    dve.wait_ge(w_lo, c - 1)
                dve.wait_ge(dq_bc, c + 1)
                st.wait()
                w = chunk_of(wf[:, c % 2, :], c)
                st.did(nc.vector.scalar_tensor_tensor(out=w, in0=chunk_of(raw[:, c % 4, :], c), scalar=1.0,
                                                      in1=chunk_of(z_ps, c), op0=ALU.subtract,
                                                      op1=ALU.subtract))
                st.wait()
                nc.vector.tensor_tensor(w, w, chunk_of(s_ps, c), ALU.mult).then_inc(dq_mul, 1)

            def h_mul(s, j):
                n = NJ * s + j
                dve.wait_ge(up_ok, n + 1)
                dve.wait_ge(sil_ok, n + 1)
                if n >= 2:
                    dve.wait_ge(h_hi, n - 1)
                nc.vector.tensor_tensor(hf[0:jw(j), n % 2, :], sil[0:jw(j), n % 2, :],
                                        up_ps[0:jw(j), :], ALU.mult).then_inc(h_ok, 1)

            def h_low(s, j):
                n = NJ * s + j
                dve.wait_ge(h_hi, n + 1)
                nc.vector.tensor_tensor(hs[0:jw(j), n % 2, 1, :], hf[0:jw(j), n % 2, :],
                                        hs[0:jw(j), n % 2, 0, :].bitcast(F32), ALU.subtract)\
                    .then_inc(h_lo, 1)

            def ffn_out(s):
                dve.wait_ge(down_ok, NJ * (s + 1))
                for t in range(4):
                    r = x[:, 4 * (s % 2) + t, :]
                    nc.vector.scalar_tensor_tensor(out=r, in0=acc[t][:, :], scalar=0.5, in1=r,
                                                   op0=ALU.mult, op1=ALU.add).then_inc(x_upd, 1)

            nc.vector.memset(gu_cols(sraw[0:96, :], early_gu), 0.0).then_inc(zeroed_a, 1)
            nc.vector.memset(sraw[0:96, 2 * F:RC], 0.0).then_inc(zeroed_a, 1)
            dve.wait_ge(pool_step, 1)
            st.did(nc.vector.tensor_scalar(shifts[:, :], pid[:, 0:1], 7, 2, ALU.bitwise_and,
                                           ALU.logical_shift_left))
            st.did(nc.vector.tensor_scalar(pid[:, 1:2], pid[:, 0:1], 31, None, ALU.bitwise_and))
            st.did(nc.vector.tensor_scalar(pid[:, 2:3], pid[:, 0:1], 63, 4, ALU.bitwise_and,
                                           ALU.logical_shift_right))
            st.wait()
            nc.vector.tensor_copy(row32[:, :], pid[:, 1:2]).then_inc(rows_ok, 1)
            st.did(nc.vector.tensor_copy(hsel[:, :], pid[:, 2:3]))
            st.wait()
            for h in range(4):
                st.did(nc.vector.tensor_scalar(headmask[:, h:h + 1], hsel[:, :], float(h), None,
                                               ALU.is_equal))
            dve.wait_ge(z_in, 32)
            z = zint[96:128, :].rearrange("p (w e) -> p w e", e=8)
            for e in range(8):
                nc.vector.tensor_scalar(z[:, :, e], zraw[96:128, :], 4 * e, 15,
                                        ALU.logical_shift_right, ALU.bitwise_and).then_inc(z_unpacked, 1)
            dve.wait_ge(sa_in, 96)
            for rows in (96, 64, 32):
                for cols in (lambda t: gu_cols(t, early_gu), lambda t: t[:, 2 * F:RC]):
                    ins = nc.vector.tensor_copy(cols(table[0:rows, :]), cols(sraw[0:rows, :]))
                    if rows == 32:
                        ins.then_inc(s_early, 1)
                    else:
                        st.did(ins)
                if rows > 32:
                    st.wait()
                    for cols in (lambda t: gu_cols(t, early_gu), lambda t: t[:, 2 * F:RC]):
                        st.did(nc.vector.tensor_tensor(cols(sraw[0:rows - 32, :]), cols(sraw[0:rows - 32, :]),
                                                       cols(table[0:rows - 32, :]), ALU.subtract))
                    st.wait()
            dve.wait_ge(gi_in, 32)
            gi, gf = gint[:, 0:D], gflt[:, 0:D]
            dve.wait_ge(rows_ok, 1)
            st.did(nc.vector.tensor_scalar(gf, gi, 0.0, float(G_GU), ALU.is_lt, ALU.mult))
            st.wait()
            st.did(nc.vector.tensor_tensor(gf, gf, gi, ALU.add))
            st.wait()
            st.did(nc.vector.tensor_scalar(gf, gf, float(G_GU - 1), 0.0, ALU.min, ALU.max))
            st.wait()
            nc.vector.tensor_scalar(onehot[:, 0:D], gf, row32[:, :], None, ALU.is_equal).then_inc(oh_gu, 1)
            for t in range(4):
                dve.wait_ge(x_in_s[t], 16)
            moments(range(4))
            rstds(0)
            ffn_xn(0, 0)
            ffn_xn(0, 1)
            for t in range(4):
                xt_low(0, t)
                if t < 2:
                    ffn_xn(0, t + 2)
            dequant(0)
            for r in range(2):
                dequant(1 + r)
                dve.wait_ge(s_conv, r + 1)
                rows = 64 - 32 * r
                cols = gu_cols(sraw[0:rows, :], slice(EARLY, F))
                nc.vector.tensor_tensor(cols, cols, gu_cols(table[0:rows, :], slice(EARLY, F)),
                                        ALU.subtract).then_inc(s_sub, 1)
            for t in range(4):
                dve.wait_ge(x_in_s[4], 64)
            for j in range(NJ):
                if j + 1 < NJ:
                    dequant(3 * j + 3)
                    dequant(3 * j + 4)
                h_mul(0, j)
                if j + 1 < NJ:
                    dequant(3 * j + 5)
                h_low(0, j)
                if j == NJ - 3:
                    moments(range(4, 6))
                if j == NJ - 2:
                    moments(range(6, 8))
                    rstds(1)
                    ffn_xn(1, 0)
                    ffn_xn(1, 1)
            for t in range(4):
                xt_low(1, t)
                if t < 2:
                    ffn_xn(1, t + 2)
            ffn_out(0)
            for j in range(NJ):
                h_mul(1, j)
                h_low(1, j)
                if j == 2:
                    dve.wait_ge(x_upd, 4)
                    moments(range(4))
                if j == 3:
                    rstds(0)
                    for t in range(2):
                        xn_tile(tile_no("attn", 0, t), t)

            def k_low(b):
                if b == 0:
                    dve.wait_ge(vp_set, 2)
                dve.wait_ge(a_khi, 4 * b + 4)
                for kt in range(2):
                    v4 = bank[6][:, S + kt * HD * 4:S + (kt + 1) * HD * 4].rearrange("p (h n) -> p h n", h=4)
                    nc.vector.tensor_copy(strips[:, b % 2, kt, :, 0:HD], v4).then_inc(a_vp, 1)
                for h in range(4):
                    nc.vector.scalar_tensor_tensor(out=kp[:, b % 2, 1, h, :], in0=bank[6][:, 0:S],
                                                   scalar=headmask[:, h:h + 1],
                                                   in1=kp[:, b % 2, 0, h, :].bitcast(F32),
                                                   op0=ALU.mult, op1=ALU.subtract).then_inc(a_klo, 1)

            def q_low(b, i):
                dve.wait_ge(a_qhi, NG * b + 4 * i + 4)
                for g in range(4 * i, 4 * i + 4):
                    src = bank[7 - i][64 * (g % 2):64 * (g % 2) + 64, (g // 2 % 2) * S:(g // 2 % 2 + 1) * S]
                    nc.vector.scalar_tensor_tensor(out=qp[64:128, b % 2, g, :], in0=src, scalar=HD ** -0.5,
                                                   in1=qp[0:64, b % 2, g, :].bitcast(F32),
                                                   op0=ALU.mult, op1=ALU.subtract).then_inc(a_qlo, 1)

            def attn_out(b, t):
                dve.wait_ge(a_y, 2 * b + t + 1)
                r = x[:, 2 * b + t, :]
                nc.vector.tensor_tensor(r, bank[6 + t][:, :], r, ALU.add).then_inc(a_x, 1)

            k_low(0)
            q_low(0, 0)
            q_low(0, 1)
            ffn_out(1)

            def masked(n):
                g, u = divmod(n, 3)
                dve.wait_ge(a_s, n + 1)
                if n >= 4:
                    dve.wait_ge(a_pt, n - 3)
                heads, w = (4, P) if u == 0 else (2, S)
                d = dist[:, 0, :] if u == 0 else dist[:, 1:3, :].rearrange("p a b -> p (a b)")
                for h in range(heads):
                    slope = SLOPES[4 * (g % NG) + (h if u == 0 else 2 * u - 2 + h)]
                    ins = nc.vector.scalar_tensor_tensor(
                        out=sc[:, n % 4, h * w:(h + 1) * w], in0=d, scalar=slope,
                        in1=bank[n % 2][:, h * w:(h + 1) * w], op0=ALU.mult, op1=ALU.add)
                ins.then_inc(a_sb, 1)
                dve.wait_ge(a_sb, n + 1)
                nc.vector.tensor_reduce(nmax[:, n % 4, 0:heads],
                                        sc[:, n % 4, :].rearrange("p (h n) -> p h n", h=heads),
                                        AX_X, ALU.max, negate=True).then_inc(a_max, 1)

            def normalise(g):
                o, b = bank[4 + g % 2], g // NG
                dve.wait_ge(a_pv, g + 1)
                if g >= 1:
                    dve.wait_ge(a_norm, 2 * g)
                nc.vector.reciprocal(rden[0:64, :], o[64:128, 0:S]).then_inc(a_norm, 1)
                dve.wait_ge(a_norm, 2 * g + 1)
                r = 64 * (g % 2)
                nc.vector.tensor_tensor(at_t[r:r + 64, b % 2, g % NG // 2, :], o[0:64, 0:S], rden[0:64, :],
                                        ALU.mult).then_inc(a_norm, 1)

            def between(m):
                b, g = divmod(m, NG)
                if b >= 1 and g in (2, 3):
                    attn_out(b - 1, g - 2)
                if b + 1 < B:
                    if g == 5:
                        k_low(b + 1)
                    if g in (6, 7):
                        q_low(b + 1, g - 6)
                    if g == 2:
                        for t in range(2):
                            xn_tile(tile_no("attn", b + 1, t), 2 * b + 2 + t)
                else:
                    if g == 2:
                        ffn_xn(2, 0)
                        ffn_xn(2, 1)
                    if g in (4, 6):
                        xt_low(2, g - 4)
                        xt_low(2, g - 3)
                    if g == 4:
                        ffn_xn(2, 2)
                        ffn_xn(2, 3)
                if b == 0 and g in (1, 4):
                    if g == 1:
                        dve.wait_ge(x_upd, 8)
                    moments(range(4, 6) if g == 1 else range(6, 8))
                if (b, g) == (1, 0):
                    rstds(1)
                if (b, g) == (2, 4):
                    dve.wait_ge(a_x, 4)
                    moments(range(0, 2))
                if (b, g) == (3, 0):
                    moments(range(2, 4))
                if (b, g) == (3, 1):
                    rstds(0)

            for n in range(3):
                masked(n)
            for m in range(LAST + 1):
                for u in range(3):
                    if m < LAST:
                        masked(3 * m + 3 + u)
                    if u == 0:
                        if m >= 2:
                            normalise(m - 2)
                        between(m)
            normalise(LAST - 1)
            normalise(LAST)
            attn_out(B - 1, 0)
            attn_out(B - 1, 1)

            for j in range(NJ):
                h_mul(2, j)
                h_low(2, j)
                if j == NJ - 4:
                    dve.wait_ge(a_x, TT)
                    moments(range(4, 8))
                if j == NJ - 3:
                    rstds(1)
                    ffn_xn(3, 0)
                    ffn_xn(3, 1)
            for t in range(4):
                xt_low(3, t)
                if t < 2:
                    ffn_xn(3, t + 2)
            ffn_out(2)
            for j in range(NJ):
                h_mul(3, j)
                h_low(3, j)
            ffn_out(3)

        @block.tensor
        def _(pe):
            def transposes(n, ps):
                pe.wait_ge(xn_ok, n + 1)
                for k in range(KT):
                    ins = nc.tensor.transpose(ps[:, k * P:(k + 1) * P], xn[:, n % 2, k * P:(k + 1) * P],
                                              ident[:, :])
                ins.then_inc(tr_ok, 1)

            def ffn_transposes(s, t):
                if t >= 2:
                    pe.wait_ge(xt_lo, 4 * s + t - 1)
                transposes(tile_no("ffn", s, t), bank[6 + t % 2])

            def broadcasts(c):
                j, kind = divmod(c, 3)
                if c == 2:
                    pe.wait_ge(oh_d, 1)
                if c == 6:
                    pe.wait_ge(s_conv, 3)
                    pe.wait_ge(z_tab, 3)
                if c >= 1:
                    pe.wait_ge(dq_mul, c)
                for ps, lo, hi in ((z_ps, 96, 128), (s_ps, 0, 96)):
                    if kind == 2:
                        ins = nc.tensor.matmul(ps[0:jw(j), :], onehot[lo:hi, D + j * P:D + j * P + jw(j)],
                                               table[lo:hi, 2 * F:RC], start=True, stop=True)
                    else:
                        for k in range(2):
                            kt = 2 * kind + k
                            ins = nc.tensor.matmul(
                                ps[:, 2 * k * jw(j):2 * (k + 1) * jw(j)].rearrange("p (g n) -> p g n", g=2),
                                onehot[lo:hi, kt * P:(kt + 1) * P],
                                gu_cols(table[lo:hi, :], slice(j * P, j * P + jw(j))), start=True, stop=True)
                ins.then_inc(dq_bc, 1)

            PARTS = ((0, 0), (1, 0), (0, 1))

            def gate_up(s, j, gu):
                n = NJ * s + j
                if j == 0 and gu == 0:
                    pe.wait_ge(xt_hi, 4 * (s + 1))
                    pe.wait_ge(xt_lo, 4 * (s + 1))
                if s == 0 and gu == 0:
                    pe.wait_ge(w_hi, 3 * j + 2)
                    pe.wait_ge(w_lo, 3 * j + 2)
                if s == 2 and j == JA and gu == 0:
                    pe.wait_ge(refilled, 16)
                if s == 2 and j == 0:
                    pe.wait_ge(a_norm, 2 * (LAST + gu))
                if n >= 1:
                    pe.wait_ge(*((sil_ok, n) if gu == 0 else (h_ok, n)))
                ps = (gate_ps, up_ps)[gu]
                for k in range(KT):
                    for q, (a, b) in enumerate(PARTS):
                        ins = nc.tensor.matmul(ps[0:jw(j), :], w_gu(a, k, gu, j), xt[:, b, k, :],
                                               start=(k == 0 and q == 0), stop=(k == KT - 1 and q == 2))
                ins.then_inc((gate_ok, up_ok)[gu], 1)

            def down(s, j):
                n = NJ * s + j
                pe.wait_ge(h_hi, n + 1)
                pe.wait_ge(h_lo, n + 1)
                if s == 0:
                    pe.wait_ge(w_hi, 3 * j + 3)
                    pe.wait_ge(w_lo, 3 * j + 3)
                if s in (1, 3) and j == 0:
                    pe.wait_ge(x_upd, 4 * s)
                for t in range(4):
                    for q, (a, b) in enumerate(PARTS):
                        ins = nc.tensor.matmul(acc[t][:, :], hs[0:jw(j), n % 2, a, t * P:(t + 1) * P],
                                               w_d[0:jw(j), b, j, :],
                                               start=(j == 0 and q == 0), stop=(j == NJ - 1 and q == 2))
                ins.then_inc(down_ok, 1)

            def project_kv(b):
                pe.wait_ge(a_xt, 2 * b + 2)
                if b == 0:
                    pe.wait_ge(aw_in, 16 * (KT + 3))
                for k in range(KT):
                    nc.tensor.matmul(bank[6][:, 0:S], wqkv[:, k, D:D + 8 * HD], xa[:, k, :], start=(k == 0),
                                     stop=(k == KT - 1))
                for kt in range(2):
                    for k in range(KT):
                        v_cols = wqkv[:, k, D + 8 * HD:D + 9 * HD].unsqueeze(1).to_broadcast([P, 4, HD])
                        o = bank[6][:, S + kt * 4 * HD:S + (kt + 1) * 4 * HD].rearrange(
                            "p (h n) -> p h n", h=4)
                        ins = nc.tensor.matmul(o, xa[:, k, kt * P:(kt + 1) * P], v_cols,
                                               start=(k == 0), stop=(k == KT - 1))
                ins.then_inc(a_kv, 1)

            def project_q(b, i):
                if i == 1:
                    pe.wait_ge(a_klo, 4 * b + 4)
                    pe.wait_ge(a_vp, 2 * b + 2)
                for m in (2 * i, 2 * i + 1):
                    for k in range(KT):
                        ins = nc.tensor.matmul(bank[7 - i][:, (m % 2) * S:(m % 2 + 1) * S],
                                               wqkv[:, k, m * P:(m + 1) * P], xa[:, k, :],
                                               start=(k == 0), stop=(k == KT - 1))
                ins.then_inc(a_q, 1)

            def scores(n):
                g, u = divmod(n, 3)
                b = g // NG
                if n < 2:
                    pe.wait_ge(x_upd, 4 + n + 1)
                else:
                    pe.wait_ge(a_sb, n - 1)
                if u == 0:
                    pe.wait_ge(a_qlo, g + 1)
                    if g % NG == 0:
                        pe.wait_ge(a_klo, 4 * b + 4)
                for part in range(2):
                    if u == 0:
                        q, k = qp[:, b % 2, g % NG, 0:P], kp[:, b % 2, part, :, 0:P]
                    else:
                        q, k = qp[:, b % 2, g % NG, P:S], kp[:, b % 2, part, 2 * u - 2:2 * u, :]
                    ins = nc.tensor.matmul(bank[n % 2][:, :].rearrange("p (h n) -> p h n", h=k.shape[1]),
                                           q, k, start=(part == 0), stop=(part == 1))
                ins.then_inc(a_s, 1)

            def exp_transposes(n):
                pe.wait_ge(a_exp, n + 1)
                if n >= 2:
                    pe.wait_ge(a_ptc, n - 1)
                for i in range(4):
                    ins = nc.tensor.transpose(bank[2 + n % 2][:, i * P:(i + 1) * P],
                                              sc[:, n % 4, i * P:(i + 1) * P], ident[:, :])
                ins.then_inc(a_pt, 1)

            def weighted_values(g):
                pe.wait_ge(a_ptc, 3 * g + 3)
                b = g // NG
                if g % NG == 0:
                    pe.wait_ge(a_vp, 2 * b + 2)
                if g >= 2:
                    pe.wait_ge(a_norm, 2 * (g - 1))
                o = bank[4 + g % 2]
                for h in range(4):
                    e = 3 * P * h
                    nc.tensor.matmul(o[:, 0:S], vp[:, b % 2, 0, h * P:(h + 1) * P], pt[:, g % 2, e:e + S],
                                     start=(h == 0), stop=False, skip_group_check=True)
                    ins = nc.tensor.matmul(o[:, P:S], vp[:, b % 2, 1, h * P:(h + 1) * P],
                                           pt[:, g % 2, e + S:e + S + P], start=False, stop=(h == 3),
                                           skip_group_check=True)
                ins.then_inc(a_pv, 1)

            def project_out(b, t):
                pe.wait_ge(a_norm, 2 * NG * (b + 1))
                for k in range(KT):
                    ins = nc.tensor.matmul(bank[6 + t][:, :], at_t[:, b % 2, k, t * P:(t + 1) * P],
                                           wo[:, k, :], start=(k == 0), stop=(k == KT - 1))
                ins.then_inc(a_y, 1)

            def extra(m):
                b, g = divmod(m, NG)
                if b >= 1 and g in (1, 2):
                    project_out(b - 1, g - 1)
                if b + 1 < B:
                    if g == 3:
                        for t in range(2):
                            if b >= 1:
                                pe.wait_ge(a_x, 2 * b)
                            transposes(tile_no("attn", b + 1, t), bank[6 + t])
                    if g == 4:
                        project_kv(b + 1)
                    if g in (5, 6):
                        project_q(b + 1, g - 5)
                elif g in (3, 5):
                    if g == 3:
                        pe.wait_ge(a_x, 2 * b)
                    ffn_transposes(2, g - 3)
                    ffn_transposes(2, g - 2)

            pe.wait_ge(consts, 1)
            for t in range(2):
                ffn_transposes(0, t)
            pe.wait_ge(s_early, 2)
            pe.wait_ge(z_tab, 2)
            pe.wait_ge(oh_gu, 1)
            for t in range(2, 4):
                ffn_transposes(0, t)
            pe.wait_ge(xt_lo, 4)
            for c in range(3):
                broadcasts(c)
            for j in range(NJ):
                if j + 1 < NJ:
                    broadcasts(3 * j + 3)
                gate_up(0, j, 0)
                if j + 1 < NJ:
                    broadcasts(3 * j + 4)
                gate_up(0, j, 1)
                if j + 1 < NJ:
                    broadcasts(3 * j + 5)
                else:
                    ffn_transposes(1, 0)
                    ffn_transposes(1, 1)
                if j >= 1:
                    down(0, j - 1)
            ffn_transposes(1, 2)
            ffn_transposes(1, 3)
            down(0, NJ - 1)
            for j in range(NJ):
                gate_up(1, j, 0)
                if j == 5:
                    for t in range(2):
                        transposes(tile_no("attn", 0, t), bank[6 + t])
                gate_up(1, j, 1)
                if j == NJ - 1:
                    project_kv(0)
                    project_q(0, 0)
                if j >= 1:
                    down(1, j - 1)
            project_q(0, 1)
            down(1, NJ - 1)

            pe.wait_ge(consts, 3)
            for n in range(3):
                scores(n)
            for m in range(LAST + 1):
                for u in range(3):
                    if m < LAST:
                        scores(3 * m + 3 + u)
                    exp_transposes(3 * m + u)
                if m >= 1:
                    weighted_values(m - 1)
                extra(m)
            weighted_values(LAST)
            gate_up(2, 0, 0)
            project_out(B - 1, 0)
            project_out(B - 1, 1)
            gate_up(2, 0, 1)
            for j in range(1, NJ):
                gate_up(2, j, 0)
                gate_up(2, j, 1)
                if j == NJ - 1:
                    pe.wait_ge(a_x, TT)
                    ffn_transposes(3, 0)
                    ffn_transposes(3, 1)
                down(2, j - 1)
            ffn_transposes(3, 2)
            ffn_transposes(3, 3)
            down(2, NJ - 1)
            for j in range(NJ):
                gate_up(3, j, 0)
                gate_up(3, j, 1)
                if j >= 1:
                    down(3, j - 1)
            down(3, NJ - 1)


_INS = ["L0_attn_hidden_states", "L0_attn_Wqkv", "L0_attn_Wo", "L0_ffn_qweight_gu", "L0_ffn_qzeros_gu",
        "L0_ffn_scales_gu", "L0_ffn_g_idx_gu", "L0_ffn_qweight_down", "L0_ffn_qzeros_down",
        "L0_ffn_scales_down", "L0_ffn_g_idx_down"]


def kernel(**inputs):
    import concourse.bacc as bacc
    from concourse.bass_utils import run_bass_kernel_spmd

    nc = bacc.Bacc("TRN2", target_bir_lowering=False, num_devices=1)
    arrays, args = {}, []
    for name in _INS:
        a = np.ascontiguousarray(inputs[name])
        if a.dtype == np.uint32:
            a = a.view(np.int32)
        arrays[f"in_{name}"] = a
        args.append(nc.dram_tensor(f"in_{name}", a.shape, mybir.dt.from_np(a.dtype), kind="ExternalInput").ap())
    shape = inputs["L0_attn_hidden_states"].shape
    out = nc.dram_tensor("out", shape, F32, kind="ExternalOutput").ap()
    macaron_block(nc, *args, out)
    r = run_bass_kernel_spmd(nc, [arrays], core_ids=[0])
    return r.results[0]["out"]
```

```python
from contextlib import ExitStack

import numpy as np

import concourse.bass as bass
from concourse import mybir

F32 = mybir.dt.float32
F32R = mybir.dt.float32r
BF16 = mybir.dt.bfloat16
I32 = mybir.dt.int32
ALU = mybir.AluOpType
ACT = mybir.ActivationFunctionType
AX_X = mybir.AxisListType.X

P = 128
EPS = 1e-5


def alibi_slopes(n):
    cp2 = 2 ** int(np.floor(np.log2(n)))
    base = 2.0 ** (-2.0 ** (-(np.log2(cp2) - 3)))
    return [float(np.float32(v)) for v in base ** np.arange(1, n + 1, dtype=np.float64)]


class Steps:

    def __init__(self, eng, sem, base=0):
        self.eng, self.sem, self.base, self.n = eng, sem, base, 0

    def did(self, ins):
        ins.then_inc(self.sem, 1)
        self.n += 1

    def wait(self):
        self.eng.wait_ge(self.sem, self.base + self.n)


def macaron_block(nc, x_in, w_qkv, w_o, qw_gu, qz_gu, sc_gu, gi_gu, qw_d, qz_d, sc_d, gi_d, out):
    B, S, D = x_in.shape
    T = B * S
    HD = (w_qkv.shape[1] - D) // 2
    NH = D // HD
    F = qw_d.shape[0] * 8
    G_GU, G_D = sc_gu.shape[0], sc_d.shape[0]
    TT = T // P
    KT = D // P
    NJ = (F + P - 1) // P
    HALF = 4 * P
    NHALF = T // HALF
    JA = 3
    FA, FB = JA * P, F - JA * P
    NG = NH // 4
    SLOPES = alibi_slopes(NH)
    RC = 2 * F + D
    KC = D + F
    NEAR = 3 * P
    assert (D, HD, S, TT % 4, NHALF) == (512, 16, 2 * P, 0, 2)

    def jw(j):
        return min(P, F - j * P)

    x_tiles = x_in.rearrange("b (t p) d -> (b t) p d", p=P)
    out_tiles = out.rearrange("b (t p) d -> (b t) p d", p=P)
    spill = nc.dram_tensor("gate_up_tail", (P, 2 * KT * 2 * FB), F32, kind="Internal").ap()

    at = [(nc.sbuf_base + 31) // 32 * 32]

    def place(name, shape, dt, size):
        t = nc.alloc_sbuf_tensor_at(name, shape, dt, offset=at[0])
        n = int(np.prod(shape[1:])) * size
        at[0] += (n + 31) // 32 * 32
        return t

    x = place("x", [P, TT, D], F32, 4)
    w_a = place("w_a", [P, 2, KT, 2, FA], F32R, 4)
    w_d = place("w_d", [P, 2, NJ, D], F32R, 4)
    xt = place("xt", [P, 2, KT, HALF], F32R, 4)
    xn = place("xn", [P, 2, D], F32, 4)
    ident = place("ident", [P, P], F32, 4)
    dist = place("dist", [P, 3, P], F32, 4)
    pid = place("pid", [P, 4], I32, 4)
    shifts = place("shifts", [P, 1], I32, 4)
    row32 = place("row32", [P, 2], F32, 4)
    headmask = place("headmask", [P, 2], F32, 4)
    hsel = place("hsel", [P, 1], F32, 4)
    stats = place("stats", [P, 4, 6], F32, 4)
    mv = place("mv", [P, TT, 2], F32, 4)
    rstd = place("rstd", [P, TT], F32, 4)
    nwt = place("nwt", [P, 2, 4], F32, 4)
    nmax = place("nmax", [P, 4, 4], F32, 4)
    dq_at = at[0]
    table = place("table", [P, RC], BF16, 2)
    onehot = place("onehot", [P, KC], BF16, 2)
    raw = place("raw", [P, 4, 512], I32, 4)
    wf = place("wf", [P, 2, 512], F32, 4)
    ff_at = at[0] = max(at[0], dq_at + 4 * (KT * (D + 9 * HD) + KT * D + KT * S))
    sil = place("sil", [P, 2, HALF], F32, 4)
    hf = place("hf", [P, 2, HALF], F32, 4)
    hs = place("hs", [P, 2, 2, HALF], F32R, 4)
    tail_at = at[0]
    w_b = place("w_b", [P, 2, KT, 2, FB], F32R, 4)
    top = at[0]
    at[0] = tail_at
    sraw = place("sraw", [P, RC], F32, 4)
    zint = place("zint", [P, RC], I32, 4)
    zraw = place("zraw", [P, RC // 8], I32, 4)
    gint = place("gint", [P, KC], I32, 4)
    gflt = place("gflt", [P, KC], F32, 4)
    assert at[0] <= top
    at[0] = dq_at
    wqkv = place("wqkv", [P, KT, D + 9 * HD], F32, 4)
    wo = place("wo", [P, KT, D], F32, 4)
    xa = place("xa", [P, KT, S], F32, 4)
    assert at[0] <= ff_at
    at[0] = ff_at
    sc = place("sc", [P, 4, 4 * P], F32, 4)
    at_t = place("at_t", [P, 2, KT, S], F32, 4)
    assert at[0] <= tail_at
    qp = place("qp", [P, 2, NH // 2, S], F32R, 4)
    kp = place("kp", [P, 2, 2, S], F32R, 4)
    vp = place("vp", [P, 2, 2, 4 * (64 + HD)], F32, 4)
    pt = place("pt", [P, 2, 12 * P], F32, 4)
    rden = place("rden", [P, 2, S], F32, 4)
    sums = place("sums", [P, 2, 8], F32, 4)
    inv = place("inv", [P, 2, 8], F32, 4)
    inv16 = place("inv16", [P, 2, 8, HD], F32, 4)
    assert at[0] <= top, (at[0], top)
    assert top <= nc.sbuf_usable_end, (top, nc.sbuf_usable_end)

    ctx = ExitStack()
    with ctx:
        bank = [ctx.enter_context(nc.psum_tensor(f"bank{n}", [P, 512], F32)) for n in range(8)]
        acc = bank[0:4]
        gate_ps, up_ps, z_ps, s_ps = bank[4], bank[5], bank[6], bank[7]

        def sem(name):
            return ctx.enter_context(nc.semaphore(name))

        x_in_s = [sem(f"x_loaded{n}") for n in range(5)]
        z_in = sem("zeros_loaded")
        gi_in = sem("gate_up_groups_loaded")
        gi_d_in = sem("down_groups_loaded")
        sa_in = sem("scales_near_loaded")
        sb_in = sem("scales_far_loaded")
        raw_in = [sem(f"raw_loaded{n}") for n in range(4)]
        aw_in = sem("attn_weights_loaded")
        zeroed = sem("load_buffers_zeroed")
        zeroed_a = sem("near_scales_zeroed")
        consts = sem("consts_ready")
        rows_ok = sem("row_numbers_ready")
        pool_step = sem("pool_step")
        dve_step = sem("dve_step")
        z_unpacked = sem("zeros_unpacked")
        z_tab = sem("zeros_in_table")
        s_first = sem("first_scales_in_table")
        near_conv = sem("near_scale_part_converted")
        near_sub = sem("near_scale_remainder")
        far_conv = sem("far_scale_part_converted")
        far_sub = sem("far_scale_remainder")
        oh_gu = sem("onehot_gate_up_ready")
        oh_d = sem("onehot_down_ready")
        dq_bc = sem("dq_broadcast")
        dq_mul = sem("dq_weight")
        w_hi = sem("w_hi_ready")
        w_lo = sem("w_lo_ready")
        spilled = sem("tail_spilled")
        refilled = [sem(f"tile{j}_refilled") for j in range(JA, NJ)]
        xn_ok = sem("xn_ready")
        tr_ok = sem("xn_transposed")
        xt_hi = sem("xt_hi_ready")
        xt_lo = sem("xt_lo_ready")
        gate_ok = sem("gate_done")
        up_ok = sem("up_done")
        sil_ok = sem("silu_done")
        h_ok = sem("h_done")
        h_hi = sem("h_hi_ready")
        h_lo = sem("h_lo_ready")
        down_ok = sem("down_done")
        sum_ok = sem("token_tile_summed")
        x_upd = sem("x_updated")
        vp_set = sem("v_blocks_set")
        a_xt = sem("attn_xt_ready")
        a_kv = sem("kv_projected")
        a_q = sem("q_projected")
        a_qhi = sem("q_hi_ready")
        a_qlo = sem("q_lo_ready")
        a_qdup = [sem(f"q_rows_repeated{i}") for i in range(2)]
        a_khi = sem("k_hi_padded")
        a_klo = sem("k_lo_padded")
        a_vp = sem("v_padded")
        a_s = sem("scores_done")
        a_sb = sem("scores_biased")
        a_max = sem("max_ready")
        a_exp = sem("exp_done")
        a_pt = sem("exp_transposed")
        a_ptc = sem("exp_t_copied")
        a_pv = sem("pv_done")
        a_inv = sem("sums_inverted")
        a_inv16 = sem("inverses_copied")
        a_rden = sem("inverses_transposed")
        a_norm = sem("attn_normed")
        a_y = sem("attn_projected")
        a_x = sem("attn_x_updated")
        stored = sem("out_stored")

        block = ctx.enter_context(nc.Block())

        NC = 3 * NJ
        LAST = NG * B - 1
        first = [lambda t: gu_cols(t, slice(0, P))]
        near = [lambda t: gu_cols(t, slice(P, NEAR)), lambda t: t[:, 2 * F:RC]]
        far = [lambda t: gu_cols(t, slice(NEAR, F))]
        strips = vp[:, :, :, :].rearrange("p b k (h n) -> p b k h n", n=64 + HD)

        def tile_no(kind, s, t):
            return {"ffn": 4 * s + t + (8 if s >= 2 else 0), "attn": 8 + 2 * s + t}[kind]

        def chunk(c):
            if c < 2:
                return 0, c
            if c == NC - 1:
                return NJ - 1, 2
            j, kind = divmod(c - 2, 3)
            return (j, 2) if kind == 2 else (j + 1, kind)

        chunk_no = {chunk(c): c for c in range(NC)}

        def q_splits(b, i):
            return 4 * (2 * b + i + 1)

        def out_bank(b, t):
            return bank[7 - t] if b < B - 2 else bank[6 + t]

        def w_gu(part, kt, gu, j):
            if j < JA:
                return w_a[:, part, kt, gu, j * P:(j + 1) * P]
            return w_b[:, part, kt, gu, (j - JA) * P:(j - JA) * P + jw(j)]

        def dq_dst(part, c):
            j, kind = chunk(c)
            if kind == 2:
                return w_d[0:jw(j), part, j, :]
            if j < JA:
                return w_a[:, part, 2 * kind:2 * kind + 2, :, j * P:(j + 1) * P]
            return w_b[:, part, 2 * kind:2 * kind + 2, :, (j - JA) * P:(j - JA) * P + jw(j)]

        def chunk_of(buf, c):
            j, kind = chunk(c)
            if kind == 2:
                return buf[0:jw(j), 0:D]
            return buf[:, 0:4 * jw(j)].rearrange("p (k g n) -> p k g n", k=2, g=2)

        def gu_cols(t, cols):
            return t[:, 0:2 * F].rearrange("p (g n) -> p g n", g=2)[:, :, cols]

        @block.sync
        def _(sp):
            def load_raw(c):
                j, kind = chunk(c)
                if c >= 4:
                    sp.wait_ge(dq_mul, c - 3)
                if kind == 2:
                    src = bass.AP(qw_d.tensor, j * (P // 8) * D, [[D, jw(j) // 8], [0, 8], [1, D]])
                    sp.dma_start(raw[0:jw(j), c % 4, :], src).then_inc(raw_in[c % 4], 16)
                    return
                for k in range(2):
                    for g in range(2):
                        row0 = (2 * kind + k) * (P // 8)
                        src = bass.AP(qw_gu.tensor, row0 * 2 * F + g * F + j * P,
                                      [[2 * F, P // 8], [0, 8], [1, jw(j)]])
                        n = (2 * k + g) * jw(j)
                        sp.dma_start(raw[:, c % 4, n:n + jw(j)], src).then_inc(raw_in[c % 4], 16)

            for t in range(4):
                sp.dma_start(x[:, t, :], x_tiles[t]).then_inc(x_in_s[t], 16)
            sp.dma_start(gint[:, D:KC], bass.AP(gi_d.tensor, 0, [[0, P], [1, F]])).then_inc(gi_d_in, 16)
            for c in range(4):
                load_raw(c)
            for t in range(4, TT):
                sp.dma_start(x[:, t, :], x_tiles[t]).then_inc(x_in_s[4], 16)
            for c in range(4, NC):
                load_raw(c)
            sp.wait_ge(w_lo, NC)
            qkv_rows = w_qkv.rearrange("(k p) n -> p k n", p=P)
            sp.dma_start(wqkv[:, :, 0:D], qkv_rows[:, :, 0:D]).then_inc(aw_in, 16)
            sp.dma_start(wqkv[:, :, D + 8 * HD:D + 9 * HD], qkv_rows[:, :, D + HD:D + 2 * HD])\
                .then_inc(aw_in, 16)
            for k in range(KT):
                src = qkv_rows[:, k, D:D + HD].unsqueeze(1).to_broadcast([P, 8, HD])
                sp.dma_start(wqkv[:, k, D:D + 8 * HD].rearrange("p (c n) -> p c n", c=8), src)\
                    .then_inc(aw_in, 16)
            sp.dma_start(wo[:, :, :], w_o.rearrange("(k p) n -> p k n", p=P)).then_inc(aw_in, 16)
            tail = w_b[:, :, :, :, :].bitcast(F32).rearrange("p a k g n -> p (a k g n)")
            sp.dma_start(spill, tail).then_inc(spilled, 16)
            sp.wait_ge(spilled, 16)
            for b in range(B):
                for i in range(2):
                    sp.wait_ge(a_qlo, q_splits(b, i))
                    if b >= 1:
                        sp.wait_ge(a_qdup[i], 16 * b)
                    rows = qp[:, b % 2, 8 * i:8 * i + 8, :].bitcast(F32)
                    sp.dma_start(rows[64:128], rows[0:64]).then_inc(a_qdup[i], 16)
            sp.wait_ge(a_pv, LAST + 1)
            sp.wait_ge(a_norm, LAST + 1)
            for j in range(JA, NJ):
                cols = slice((j - JA) * P, (j - JA) * P + jw(j))
                split = [v.rearrange("p (n c) -> p n c", c=FB)[:, :, cols] for v in (tail, spill)]
                sp.dma_start(*split).then_inc(refilled[j - JA], 16)
            for done in refilled:
                sp.wait_ge(done, 16)
            for t in range(TT):
                sp.wait_ge(x_upd, TT + t + 1)
                sp.dma_start(out_tiles[t], x[:, t, :]).then_inc(stored, 16)
            sp.wait_ge(stored, 16 * TT)

        @block.gpsimd
        def _(pool):
            st = Steps(pool, pool_step)
            st.did(nc.gpsimd.iota(pid[:, 0:1], [[0, 1]], base=0, channel_multiplier=1))
            nc.gpsimd.memset(zraw[:, :], 0).then_inc(zeroed, 1)
            nc.gpsimd.memset(gu_cols(sraw[0:32, :], slice(NEAR, F)), 0.0).then_inc(zeroed, 1)
            st.did(nc.gpsimd.memset(ident[:, :], 0.0))
            st.did(nc.gpsimd.iota(dist[:, 0, :], [[1, P]], base=0, channel_multiplier=-1,
                                  allow_small_or_imprecise_dtypes=True))
            st.did(nc.gpsimd.iota(dist[:, 1:3, :], [[P, 2], [1, P]], base=-P, channel_multiplier=-1,
                                  allow_small_or_imprecise_dtypes=True))
            st.wait()
            nc.gpsimd.affine_select(out=ident[:, :], in_=ident[:, :], compare_op=ALU.not_equal, fill=1.0,
                                    base=0, pattern=[[-1, P]], channel_multiplier=1).then_inc(consts, 1)
            for n in (0, 2):
                nc.gpsimd.affine_select(out=dist[:, n, :], in_=dist[:, n, :], compare_op=ALU.is_ge,
                                        fill=-1e33, base=0, pattern=[[-1, P]],
                                        channel_multiplier=1).then_inc(consts, 1)
            pool.wait_ge(gi_d_in, 16)
            pool.wait_ge(rows_ok, 2)
            gi, gf = gint[:, D:KC], gflt[:, D:KC]
            st.did(nc.gpsimd.tensor_scalar(gf.bitcast(I32), gi, 0.0, float(G_D), ALU.is_lt, ALU.mult))
            st.wait()
            st.did(nc.gpsimd.tensor_tensor(gi, gf.bitcast(I32), gi, ALU.add))
            st.wait()
            st.did(nc.gpsimd.tensor_scalar(gf, gi, float(G_D - 1), 0.0, ALU.min, ALU.max))
            st.wait()
            for c in range(NC):
                if c == 2:
                    nc.gpsimd.tensor_scalar(onehot[:, D:KC], gf, row32[:, 0:1], None, ALU.is_equal)\
                        .then_inc(oh_d, 1)
                pool.wait_ge(w_hi, c + 1)
                nc.gpsimd.tensor_tensor(dq_dst(1, c), chunk_of(wf[:, c % 2, :], c),
                                        dq_dst(0, c).bitcast(F32), ALU.subtract).then_inc(w_lo, 1)
            pool.wait_ge(spilled, 16)
            pool.wait_ge(up_ok, 2 * NJ)
            nc.gpsimd.memset(vp[:, :, :, :], 0.0).then_inc(vp_set, 1)

        @block.scalar
        def _(act):
            act.wait_ge(zeroed, 1)
            act.dma_start(zraw[96:96 + G_GU, 0:F // 4], qz_gu).then_inc(z_in, 16)
            act.dma_start(zraw[96:96 + G_D, F // 4:RC // 8], qz_d).then_inc(z_in, 16)
            act.dma_start(gint[:, 0:D], bass.AP(gi_gu.tensor, 0, [[0, P], [1, D]])).then_inc(gi_in, 16)
            act.wait_ge(zeroed_a, 2)
            gu3 = sc_gu.rearrange("r (g n) -> r g n", g=2)
            act.dma_start(gu_cols(sraw[0:G_GU, :], slice(0, NEAR)), gu3[:, :, 0:NEAR]).then_inc(sa_in, 16)
            act.dma_start(sraw[0:G_D, 2 * F:RC], sc_d).then_inc(sa_in, 16)
            act.wait_ge(zeroed, 2)
            act.dma_start(gu_cols(sraw[0:G_GU, :], slice(NEAR, F)), gu3[:, :, NEAR:F]).then_inc(sb_in, 16)
            act.wait_ge(z_unpacked, 8)
            nc.scalar.copy(gu_cols(table[96:128, :], slice(0, NEAR)), gu_cols(zint[96:128, :], slice(0, NEAR)))\
                .then_inc(z_tab, 1)
            nc.scalar.copy(table[96:128, 2 * F:RC], zint[96:128, 2 * F:RC]).then_inc(z_tab, 1)

            def xt_high(s, t):
                act.wait_ge(tr_ok, tile_no("ffn", s, t) + 1)
                src = bank[6 + t % 2][:, :].rearrange("p (k n) -> p k n", k=KT)
                nc.scalar.copy(xt[:, 0, :, t * P:(t + 1) * P], src).then_inc(xt_hi, 1)

            def dq_high(c):
                act.wait_ge(dq_mul, c + 1)
                nc.scalar.copy(dq_dst(0, c), chunk_of(wf[:, c % 2, :], c)).then_inc(w_hi, 1)

            def silu(s, j):
                n = NJ * s + j
                act.wait_ge(gate_ok, n + 1)
                if n >= 2:
                    act.wait_ge(h_ok, n - 1)
                nc.scalar.activation(sil[0:jw(j), n % 2, :], gate_ps[0:jw(j), :], ACT.Silu)\
                    .then_inc(sil_ok, 1)

            def h_high(s, j):
                n = NJ * s + j
                act.wait_ge(h_ok, n + 1)
                if n >= 2:
                    act.wait_ge(down_ok, n - 1)
                nc.scalar.copy(hs[0:jw(j), n % 2, 0, :], hf[0:jw(j), n % 2, :]).then_inc(h_hi, 1)

            def x_copy(b, t):
                act.wait_ge(tr_ok, tile_no("attn", b, t) + 1)
                nc.scalar.copy(xa[:, :, t * P:(t + 1) * P],
                               bank[6 + t][:, :].rearrange("p (k n) -> p k n", k=KT)).then_inc(a_xt, 1)

            def k_high(b):
                act.wait_ge(a_kv, b + 1)
                for h in range(2):
                    nc.scalar.activation(kp[0:64, b % 2, h, :], bank[6][0:64, 0:S], ACT.Copy,
                                         scale=headmask[0:64, h:h + 1]).then_inc(a_khi, 1)

            def q_high(b, i, steps=range(4)):
                act.wait_ge(a_q, 2 * b + i + 1)
                for n in steps:
                    src = bank[7 - i][32 * n:32 * n + 32, :].rearrange("p (m s) -> p m s", m=2)
                    nc.scalar.activation(qp[0:32, b % 2, 8 * i + n:8 * i + 8:4, :], src, ACT.Copy,
                                         scale=HD ** -0.5).then_inc(a_qhi, 1)

            def convert(cols, conv, sub, r):
                if r == 0:
                    act.wait_ge(*((sa_in, 32) if cols is near else (sb_in, 16)))
                else:
                    act.wait_ge(sub, r * len(cols))
                for c in cols:
                    nc.scalar.copy(c(table[64 - 32 * r:96 - 32 * r, :]), c(sraw[0:32, :])).then_inc(conv, 1)

            convert(near, near_conv, near_sub, 0)
            nc.scalar.copy(gu_cols(table[96:128, :], slice(NEAR, F)),
                           gu_cols(zint[96:128, :], slice(NEAR, F))).then_inc(z_tab, 1)
            xt_high(0, 0)
            xt_high(0, 1)
            convert(far, far_conv, far_sub, 0)
            xt_high(0, 2)
            xt_high(0, 3)
            convert(near, near_conv, near_sub, 1)
            dq_high(0)
            convert(near, near_conv, near_sub, 2)
            dq_high(1)
            convert(far, far_conv, far_sub, 1)
            for j in range(NJ):
                if j + 1 < NJ:
                    dq_high(3 * j + 2)
                silu(0, j)
                if j + 1 < NJ:
                    dq_high(3 * j + 3)
                if j + 1 < NJ:
                    h_high(0, j)
                    dq_high(3 * j + 4)
                if j == 0:
                    convert(far, far_conv, far_sub, 2)
                if j == NJ - 1:
                    dq_high(NC - 1)
                    xt_high(1, 0)
                    xt_high(1, 1)
                    h_high(0, j)
            for t in range(2, 4):
                xt_high(1, t)
            for j in range(NJ):
                silu(1, j)
                h_high(1, j)
                if j == 6:
                    act.wait_ge(w_lo, NC)
                    x_copy(0, 0)
                    x_copy(0, 1)
            act.wait_ge(spilled, 16)
            q_high(0, 0)
            k_high(0)

            def exps(n):
                act.wait_ge(a_max, n + 1)
                g, u = divmod(n, 3)
                if u == 0 and g >= 2:
                    act.wait_ge(a_inv, g - 1)
                heads, w, first = (4, P, 0) if u == 0 else (2, S, 2 + 2 * u)
                for h in range(heads):
                    r = sc[:, n % 4, h * w:(h + 1) * w]
                    ins = nc.scalar.activation(r, r, ACT.Exp, bias=nmax[:, n % 4, h:h + 1],
                                               accum_out=sums[:, g % 2, first + h:first + h + 1])
                ins.then_inc(a_exp, 1)

            def exp_t(n):
                g, u = divmod(n, 3)
                act.wait_ge(a_pt, n + 1)
                heads = pt[:, g % 2, :].rearrange("p (h n) -> p h n", h=4)
                if u == 0:
                    dst, src = heads[:, :, 0:P], bank[2 + n % 2][:, :].rearrange("p (h n) -> p h n", h=4)
                else:
                    dst = heads[:, 2 * u - 2:2 * u, P:3 * P]
                    src = bank[2 + n % 2][:, :].rearrange("p (h n) -> p h n", h=2)
                nc.scalar.copy(dst, src).then_inc(a_ptc, 1)

            def between(m, u):
                b, g = divmod(m, NG)
                if m == 0 and u >= 1:
                    q_high(0, 1, range(2 * u - 2, 2 * u))
                if b + 1 < B:
                    if m == 1 and u == 2:
                        x_copy(1, 0)
                    if m == 2 and u == 0:
                        x_copy(1, 1)
                    if b >= 1 and g == 1 and u < 2:
                        x_copy(b + 1, u)
                    if g == 3 and u == 1:
                        k_high(b + 1)
                    if g in (4, 5) and u >= 1:
                        q_high(b + 1, g - 4, range(2 * u - 2, 2 * u))
                elif g in (3, 5) and u >= 1:
                    xt_high(2, g - 3 + u - 1)

            def rden_copy(g):
                act.wait_ge(a_pv, g + 1)
                if g >= 2:
                    act.wait_ge(a_norm, g - 1)
                nc.scalar.copy(rden[0:64, g % 2, :], bank[4 + g % 2][0:64, S:2 * S]).then_inc(a_rden, 1)

            for n in range(3):
                exps(n)
            for m in range(LAST + 1):
                for u in range(3):
                    exp_t(3 * m + u)
                    if u == 0 and m >= 2:
                        rden_copy(m - 2)
                    between(m, u)
                    if m < LAST:
                        exps(3 * m + 3 + u)
            rden_copy(LAST - 1)
            rden_copy(LAST)

            for j in range(NJ):
                silu(2, j)
                h_high(2, j)
            for t in range(4):
                xt_high(3, t)
            for j in range(NJ):
                silu(3, j)
                h_high(3, j)

        @block.vector
        def _(dve):
            st = Steps(dve, dve_step)

            def moments(tiles):
                for t in tiles:
                    st.did(nc.vector.bn_stats(stats[:, t % 4, :], x[:, t, :]))
                st.wait()
                for t in tiles:
                    st.did(nc.vector.bn_aggr(mv[:, t, :], stats[:, t % 4, :]))

            def rstd_seed(half):
                a, u, y = nwt[:, 0, :], nwt[:, 1, :], rstd[:, 4 * half:4 * half + 4]
                st.wait()
                st.did(nc.vector.tensor_scalar(a, mv[:, 4 * half:4 * half + 4, 1], EPS, None, ALU.add))
                st.wait()
                st.did(nc.vector.tensor_scalar(u.bitcast(I32), a.bitcast(I32), 1, None,
                                               ALU.logical_shift_right))
                st.wait()
                st.did(nc.vector.tensor_scalar(y.bitcast(I32), u.bitcast(I32), -1.0, float(0x5f3759df),
                                               ALU.mult, ALU.add))
                st.did(nc.vector.tensor_scalar(a, a, -0.5, None, ALU.mult))

            def rstd_step(half):
                a, u, y = nwt[:, 0, :], nwt[:, 1, :], rstd[:, 4 * half:4 * half + 4]
                st.wait()
                st.did(nc.vector.tensor_tensor(u, y, y, ALU.mult))
                st.wait()
                st.did(nc.vector.tensor_tensor(u, u, a, ALU.mult))
                st.wait()
                st.did(nc.vector.scalar_tensor_tensor(out=y, in0=u, scalar=1.5, in1=y, op0=ALU.add,
                                                      op1=ALU.mult))

            def rstds(half):
                rstd_seed(half)
                for _ in range(3):
                    rstd_step(half)
                st.wait()

            def xn_tile(n, tile):
                if n >= 2:
                    dve.wait_ge(tr_ok, n - 1)
                nc.vector.tensor_scalar(xn[:, n % 2, :], x[:, tile, :], mv[:, tile, 0:1],
                                        rstd[:, tile:tile + 1], ALU.subtract, ALU.mult).then_inc(xn_ok, 1)

            def xt_low(s, t):
                dve.wait_ge(xt_hi, 4 * s + t + 1)
                src = bank[6 + t % 2][:, :].rearrange("p (k n) -> p k n", k=KT)
                nc.vector.tensor_tensor(xt[:, 1, :, t * P:(t + 1) * P], src,
                                        xt[:, 0, :, t * P:(t + 1) * P].bitcast(F32), ALU.subtract)\
                    .then_inc(xt_lo, 1)

            def ffn_xn(s, t):
                xn_tile(tile_no("ffn", s, t), 4 * (s % 2) + t)

            def dequant(c):
                j, kind = chunk(c)
                dve.wait_ge(raw_in[c % 4], sum(16 if chunk(k)[1] == 2 else 64
                                               for k in range(c % 4, c + 1, 4)))
                rows = jw(j) if kind == 2 else P
                flat = raw[0:rows, c % 4, 0:(D if kind == 2 else 4 * jw(j))]
                st.did(nc.vector.tensor_scalar(flat, flat, shifts[0:rows, :], 15,
                                               ALU.logical_shift_right, ALU.bitwise_and))
                if c >= 2:
                    dve.wait_ge(w_lo, c - 1)
                dve.wait_ge(dq_bc, c + 1)
                st.wait()
                w = chunk_of(wf[:, c % 2, :], c)
                st.did(nc.vector.scalar_tensor_tensor(out=w, in0=chunk_of(raw[:, c % 4, :], c), scalar=1.0,
                                                      in1=chunk_of(z_ps, c), op0=ALU.subtract,
                                                      op1=ALU.subtract))
                st.wait()
                nc.vector.tensor_tensor(w, w, chunk_of(s_ps, c), ALU.mult).then_inc(dq_mul, 1)

            def h_mul(s, j):
                n = NJ * s + j
                dve.wait_ge(up_ok, n + 1)
                dve.wait_ge(sil_ok, n + 1)
                if n >= 2:
                    dve.wait_ge(h_hi, n - 1)
                nc.vector.tensor_tensor(hf[0:jw(j), n % 2, :], sil[0:jw(j), n % 2, :],
                                        up_ps[0:jw(j), :], ALU.mult).then_inc(h_ok, 1)

            def h_low(s, j):
                n = NJ * s + j
                dve.wait_ge(h_hi, n + 1)
                nc.vector.tensor_tensor(hs[0:jw(j), n % 2, 1, :], hf[0:jw(j), n % 2, :],
                                        hs[0:jw(j), n % 2, 0, :].bitcast(F32), ALU.subtract)\
                    .then_inc(h_lo, 1)

            def ffn_out(s, tiles=range(4)):
                for t in tiles:
                    dve.wait_ge(*((sum_ok, 3 * s + t + 1) if t < 3 else (down_ok, NJ * (s + 1))))
                    r = x[:, 4 * (s % 2) + t, :]
                    nc.vector.scalar_tensor_tensor(out=r, in0=acc[t][:, :], scalar=0.5, in1=r,
                                                   op0=ALU.mult, op1=ALU.add).then_inc(x_upd, 1)

            nc.vector.memset(gu_cols(sraw[0:32, :], slice(0, NEAR)), 0.0).then_inc(zeroed_a, 1)
            nc.vector.memset(sraw[0:32, 2 * F:RC], 0.0).then_inc(zeroed_a, 1)
            dve.wait_ge(pool_step, 1)
            st.did(nc.vector.tensor_scalar(shifts[:, :], pid[:, 0:1], 7, 2, ALU.bitwise_and,
                                           ALU.logical_shift_left))
            st.did(nc.vector.tensor_scalar(pid[:, 1:2], pid[:, 0:1], 31, None, ALU.bitwise_and))
            st.did(nc.vector.tensor_scalar(pid[:, 2:3], pid[:, 0:1], 31, 4, ALU.bitwise_and,
                                           ALU.logical_shift_right))
            st.wait()
            for n, groups in enumerate((0, G_GU)):
                nc.vector.tensor_scalar(row32[:, n:n + 1], pid[:, 1:2], float(groups), None, ALU.add)\
                    .then_inc(rows_ok, 1)
            st.did(nc.vector.tensor_copy(hsel[:, :], pid[:, 2:3]))
            st.wait()
            for h in range(2):
                st.did(nc.vector.tensor_scalar(headmask[:, h:h + 1], hsel[:, :], float(h), None,
                                               ALU.is_equal))
            for t in range(4):
                dve.wait_ge(x_in_s[t], 16)
                st.did(nc.vector.bn_stats(stats[:, t, :], x[:, t, :]))
            st.wait()
            for t in range(4):
                st.did(nc.vector.bn_aggr(mv[:, t, :], stats[:, t, :]))
            dve.wait_ge(z_in, 32)
            z = zint[96:128, :].rearrange("p (w e) -> p w e", e=8)
            for e in range(8):
                nc.vector.tensor_scalar(z[:, :, e], zraw[96:128, :], 4 * e, 15,
                                        ALU.logical_shift_right, ALU.bitwise_and).then_inc(z_unpacked, 1)
            rstds(0)
            ffn_xn(0, 0)
            ffn_xn(0, 1)
            dve.wait_ge(gi_in, 16)
            gi, gf = gint[:, 0:D], gflt[:, 0:D]
            dve.wait_ge(rows_ok, 2)
            st.did(nc.vector.tensor_scalar(gf, gi, float(G_GU), float(2 * G_GU - 1), ALU.add, ALU.min))
            st.wait()
            st.did(nc.vector.tensor_scalar(onehot[:, 0:D], gf, 0.0, row32[:, 0:1], ALU.max, ALU.is_equal))
            st.wait()
            nc.vector.scalar_tensor_tensor(out=onehot[:, 0:D], in0=gf, scalar=row32[:, 1:2],
                                           in1=onehot[:, 0:D], op0=ALU.is_equal, op1=ALU.add)\
                .then_inc(oh_gu, 1)
            for t in range(2):
                xt_low(0, t)
                ffn_xn(0, t + 2)
            dve.wait_ge(sa_in, 32)
            for row0 in (64, 32, 0):
                ins = nc.vector.tensor_copy(first[0](table[row0:row0 + 32, :]), first[0](sraw[0:32, :]))
                if row0 == 0:
                    ins.then_inc(s_first, 1)
                else:
                    st.did(ins)
                    st.wait()
                    st.did(nc.vector.tensor_tensor(first[0](sraw[0:32, :]), first[0](sraw[0:32, :]),
                                                   first[0](table[row0:row0 + 32, :]), ALU.subtract))
                    st.wait()

            def remainder(cols, conv, sub, r):
                dve.wait_ge(conv, (r + 1) * len(cols))
                for n, c in enumerate(cols):
                    nc.vector.tensor_tensor(c(sraw[0:32, :]), c(sraw[0:32, :]),
                                            c(table[64 - 32 * r:96 - 32 * r, :]), ALU.subtract)\
                        .then_inc(sub, 1)
                    dve.wait_ge(sub, r * len(cols) + n + 1)

            remainder(near, near_conv, near_sub, 0)
            xt_low(0, 2)
            xt_low(0, 3)
            dequant(0)
            remainder(near, near_conv, near_sub, 1)
            dequant(1)
            remainder(far, far_conv, far_sub, 0)
            dve.wait_ge(x_in_s[4], 64)
            for j in range(NJ):
                dequant(3 * j + 2)
                if j == 0:
                    remainder(far, far_conv, far_sub, 1)
                if j + 1 < NJ:
                    dequant(3 * j + 3)
                else:
                    for t in range(2):
                        xt_low(1, t)
                        ffn_xn(1, t + 2)
                h_mul(0, j)
                if j + 1 < NJ:
                    dequant(3 * j + 4)
                h_low(0, j)
                if NJ - 8 <= j < NJ - 4:
                    moments(range(j - NJ + 12, j - NJ + 13))
                if j == NJ - 4:
                    rstd_seed(1)
                if j in (NJ - 4, NJ - 3):
                    rstd_step(1)
                if j == NJ - 2:
                    rstd_step(1)
                    st.wait()
                    ffn_xn(1, 0)
                    ffn_xn(1, 1)
            for t in range(2, 4):
                xt_low(1, t)
            ffn_out(0)
            for j in range(NJ):
                h_mul(1, j)
                h_low(1, j)
                if j == 2:
                    dve.wait_ge(x_upd, 4)
                    moments(range(4))
                if j == 3:
                    rstds(0)
                if j in (3, NJ - 2):
                    for t in range(2):
                        b = 0 if j == 3 else 1
                        xn_tile(tile_no("attn", b, t), 2 * b + t)

            def k_low(b):
                if b == 0:
                    dve.wait_ge(vp_set, 1)
                dve.wait_ge(a_khi, 2 * b + 2)
                for kt in range(2):
                    v4 = bank[6][:, S + kt * HD * 4:S + (kt + 1) * HD * 4].rearrange("p (h n) -> p h n", h=4)
                    nc.vector.tensor_copy(strips[:, b % 2, kt, :, 0:HD], v4).then_inc(a_vp, 1)
                for h in range(2):
                    nc.vector.scalar_tensor_tensor(out=kp[64:128, b % 2, h, :], in0=bank[6][64:128, 0:S],
                                                   scalar=headmask[64:128, h:h + 1],
                                                   in1=kp[0:64, b % 2, h, :].bitcast(F32),
                                                   op0=ALU.mult, op1=ALU.subtract).then_inc(a_klo, 1)

            def q_low(b, i, steps=range(4)):
                dve.wait_ge(a_qhi, q_splits(b, i))
                for n in steps:
                    src = bank[7 - i][32 * n:32 * n + 32, :].rearrange("p (m s) -> p m s", m=2)
                    pairs = slice(8 * i + n, 8 * i + 8, 4)
                    nc.vector.scalar_tensor_tensor(out=qp[32:64, b % 2, pairs, :], in0=src, scalar=HD ** -0.5,
                                                   in1=qp[0:32, b % 2, pairs, :].bitcast(F32),
                                                   op0=ALU.mult, op1=ALU.subtract).then_inc(a_qlo, 1)

            def attn_out(b, t):
                dve.wait_ge(a_y, 2 * b + t + 1)
                r = x[:, 2 * b + t, :]
                nc.vector.tensor_tensor(r, out_bank(b, t)[:, :], r, ALU.add).then_inc(a_x, 1)

            dve.wait_ge(spilled, 16)
            q_low(0, 0)
            k_low(0)
            ffn_out(1, range(0, 2))

            def unit(n):
                return (4, P) if n % 3 == 0 else (2, S)

            def biased(n):
                g, u = divmod(n, 3)
                dve.wait_ge(a_s, n + 1)
                if n >= 4:
                    dve.wait_ge(a_pt, n - 3)
                heads, w = unit(n)
                d = dist[:, 0, :] if u == 0 else dist[:, 1:3, :].rearrange("p a b -> p (a b)")
                for h in range(heads):
                    slope = SLOPES[4 * (g % NG) + (h if u == 0 else 2 * u - 2 + h)]
                    ins = nc.vector.scalar_tensor_tensor(
                        out=sc[:, n % 4, h * w:(h + 1) * w], in0=d, scalar=slope,
                        in1=bank[n % 2][:, h * w:(h + 1) * w], op0=ALU.mult, op1=ALU.add)
                ins.then_inc(a_sb, 1)

            def maxima(n):
                heads, w = unit(n)
                dve.wait_ge(a_sb, n + 1)
                nc.vector.tensor_reduce(nmax[:, n % 4, 0:heads],
                                        sc[:, n % 4, :].rearrange("p (h n) -> p h n", h=heads),
                                        AX_X, ALU.max, negate=True).then_inc(a_max, 1)

            def inverses(g):
                dve.wait_ge(a_exp, 3 * g + 3)
                nc.vector.reciprocal(inv[:, g % 2, :], sums[:, g % 2, :]).then_inc(a_inv, 1)

            def inverse_copies(g):
                dve.wait_ge(a_inv, g + 1)
                if g >= 2:
                    dve.wait_ge(a_pv, g - 1)
                nc.vector.tensor_copy(inv16[:, g % 2, :, :],
                                      inv[:, g % 2, :].unsqueeze(2).to_broadcast([P, 8, HD]))\
                    .then_inc(a_inv16, 1)

            def normalise(g):
                o, b = bank[4 + g % 2], g // NG
                dve.wait_ge(a_rden, g + 1)
                r = 64 * (g % 2)
                nc.vector.tensor_tensor(at_t[r:r + 64, b % 2, g % NG // 2, :], o[0:64, 0:S],
                                        rden[0:64, g % 2, :], ALU.mult).then_inc(a_norm, 1)

            def between(m, u):
                b, g = divmod(m, NG)
                if m == 1 and u < 2:
                    q_low(0, 1, range(2 * u, 2 * u + 2))
                if b >= 2 and (g, u) == (0, 0):
                    attn_out(b - 2, 1)
                if b >= 1 and (g, u) == (7, 0):
                    attn_out(b - 1, 0)
                if b + 1 < B:
                    if (g, u) == (3, 2):
                        k_low(b + 1)
                    if g in (5, 6):
                        q_low(b + 1, g - 5, (range(0, 2), range(2, 4), range(0))[u])
                if b == 0:
                    if g in (1, 2) and u < 2:
                        if (g, u) == (1, 0):
                            dve.wait_ge(x_upd, 8)
                        moments(range(2 + 2 * g + u, 3 + 2 * g + u))
                    if (g, u) == (3, 1):
                        rstd_seed(1)
                    if g == 4:
                        rstd_step(1)
                if b + 2 < B and g == 7 and u >= 1:
                    st.wait()
                    xn_tile(tile_no("attn", b + 2, u - 1), 2 * b + 4 + u - 1)
                if b == B - 2 and g == 4 and u < 2:
                    dve.wait_ge(a_x, 2)
                    moments(range(u, u + 1))
                if b == B - 1:
                    if (g, u) == (0, 1):
                        dve.wait_ge(a_x, 4)
                        moments(range(2, 4))
                    if (g, u) == (0, 2):
                        rstd_seed(0)
                    if g == 1:
                        rstd_step(0)
                    if g in (2, 3) and u < 2:
                        st.wait()
                        ffn_xn(2, 2 * g - 4 + u)
                    if (g, u) in ((3, 2), (4, 0), (5, 2), (6, 0)):
                        xt_low(2, {3: 0, 4: 1, 5: 2, 6: 3}[g])

            for n in range(3):
                biased(n)
                maxima(n)
                if n == 0:
                    ffn_out(1, range(2, 4))
            for m in range(LAST + 1):
                for u in range(3):
                    if m < LAST:
                        biased(3 * m + 3 + u)
                    if u == 0 and m >= 1:
                        inverses(m - 1)
                    if u == 1 and m >= 2:
                        normalise(m - 2)
                    if m < LAST:
                        maxima(3 * m + 3 + u)
                    if u == 0 and m >= 1:
                        inverse_copies(m - 1)
                    between(m, u)
            inverses(LAST)
            inverse_copies(LAST)
            attn_out(B - 2, 1)
            normalise(LAST - 1)
            normalise(LAST)
            attn_out(B - 1, 0)
            attn_out(B - 1, 1)

            for j in range(NJ):
                h_mul(2, j)
                h_low(2, j)
                if j == NJ - 4:
                    dve.wait_ge(a_x, TT)
                    moments(range(4, 8))
                if j == NJ - 3:
                    rstds(1)
                    ffn_xn(3, 0)
                    ffn_xn(3, 1)
            for t in range(4):
                xt_low(3, t)
                if t < 2:
                    ffn_xn(3, t + 2)
            ffn_out(2)
            for j in range(NJ):
                h_mul(3, j)
                h_low(3, j)
            ffn_out(3)

        @block.tensor
        def _(pe):
            def transposes(n, ps):
                pe.wait_ge(xn_ok, n + 1)
                for k in range(KT):
                    ins = nc.tensor.transpose(ps[:, k * P:(k + 1) * P], xn[:, n % 2, k * P:(k + 1) * P],
                                              ident[:, :])
                ins.then_inc(tr_ok, 1)

            def ffn_transposes(s, t):
                if t >= 2:
                    pe.wait_ge(xt_lo, 4 * s + t - 1)
                transposes(tile_no("ffn", s, t), bank[6 + t % 2])

            def broadcasts(c):
                j, kind = chunk(c)
                if c == chunk_no[0, 2]:
                    pe.wait_ge(oh_d, 1)
                if c == chunk_no[1, 0]:
                    pe.wait_ge(near_conv, 3 * len(near))
                if c == chunk_no[NEAR // P, 0]:
                    pe.wait_ge(far_conv, 3)
                    pe.wait_ge(z_tab, 3)
                if c >= 1:
                    pe.wait_ge(dq_mul, c)
                for ps, lo, hi in ((z_ps, 96, 128), (s_ps, 0, 96)):
                    if kind == 2:
                        ins = nc.tensor.matmul(ps[0:jw(j), :], onehot[lo:hi, D + j * P:D + j * P + jw(j)],
                                               table[lo:hi, 2 * F:RC], start=True, stop=True)
                    else:
                        for k in range(2):
                            kt = 2 * kind + k
                            ins = nc.tensor.matmul(
                                ps[:, 2 * k * jw(j):2 * (k + 1) * jw(j)].rearrange("p (g n) -> p g n", g=2),
                                onehot[lo:hi, kt * P:(kt + 1) * P],
                                gu_cols(table[lo:hi, :], slice(j * P, j * P + jw(j))), start=True, stop=True)
                ins.then_inc(dq_bc, 1)

            PARTS = ((0, 0), (1, 0), (0, 1))

            def gate_up(s, j, gu):
                n = NJ * s + j
                if j == 0 and gu == 0:
                    pe.wait_ge(xt_hi, 4 * (s + 1))
                    pe.wait_ge(xt_lo, 4 * (s + 1))
                if s == 2 and j >= JA and gu == 0:
                    pe.wait_ge(refilled[j - JA], 16)
                if s == 2 and j == 0:
                    pe.wait_ge(a_norm, LAST + gu)
                if n >= 1:
                    pe.wait_ge(*((sil_ok, n) if gu == 0 else (h_ok, n)))
                ps = (gate_ps, up_ps)[gu]
                for k in range(KT):
                    if s == 0 and gu == 0 and k % 2 == 0:
                        pe.wait_ge(w_hi, chunk_no[j, k // 2] + 1)
                        pe.wait_ge(w_lo, chunk_no[j, k // 2] + 1)
                    for q, (a, b) in enumerate(PARTS):
                        ins = nc.tensor.matmul(ps[0:jw(j), :], w_gu(a, k, gu, j), xt[:, b, k, :],
                                               start=(k == 0 and q == 0), stop=(k == KT - 1 and q == 2))
                ins.then_inc((gate_ok, up_ok)[gu], 1)

            def down(s, j):
                n = NJ * s + j
                pe.wait_ge(h_hi, n + 1)
                pe.wait_ge(h_lo, n + 1)
                if s == 0:
                    pe.wait_ge(w_hi, chunk_no[j, 2] + 1)
                    pe.wait_ge(w_lo, chunk_no[j, 2] + 1)
                if s in (1, 3) and j == 0:
                    pe.wait_ge(x_upd, 4 * s)
                for t in range(4):
                    for q, (a, b) in enumerate(PARTS):
                        ins = nc.tensor.matmul(acc[t][:, :], hs[0:jw(j), n % 2, a, t * P:(t + 1) * P],
                                               w_d[0:jw(j), b, j, :],
                                               start=(j == 0 and q == 0), stop=(j == NJ - 1 and q == 2))
                    if j == NJ - 1 and t < 3:
                        ins.then_inc(sum_ok, 1)
                ins.then_inc(down_ok, 1)

            def project_k(b):
                pe.wait_ge(a_xt, 2 * b + 2)
                for k in range(KT):
                    nc.tensor.matmul(bank[6][:, 0:S], wqkv[:, k, D:D + 8 * HD], xa[:, k, :], start=(k == 0),
                                     stop=(k == KT - 1))

            def project_v(kt):
                for k in range(KT):
                    v_cols = wqkv[:, k, D + 8 * HD:D + 9 * HD].unsqueeze(1).to_broadcast([P, 4, HD])
                    o = bank[6][:, S + kt * 4 * HD:S + (kt + 1) * 4 * HD].rearrange("p (h n) -> p h n", h=4)
                    ins = nc.tensor.matmul(o, xa[:, k, kt * P:(kt + 1) * P], v_cols,
                                           start=(k == 0), stop=(k == KT - 1))
                if kt == 1:
                    ins.then_inc(a_kv, 1)

            def project_q(b, i, steps):
                if i == 1 and steps[0] == 0:
                    pe.wait_ge(a_klo, 2 * b + 2)
                    pe.wait_ge(a_vp, 2 * b + 2)
                for n in steps:
                    m, k = divmod(n, KT)
                    ins = nc.tensor.matmul(bank[7 - i][:, m * S:(m + 1) * S],
                                           wqkv[:, k, (2 * i + m) * P:(2 * i + m + 1) * P], xa[:, k, :],
                                           start=(k == 0), stop=(k == KT - 1))
                if steps[-1] == 2 * KT - 1:
                    ins.then_inc(a_q, 1)

            def scores(n):
                g, u = divmod(n, 3)
                b = g // NG
                if n < 2:
                    pe.wait_ge(x_upd, 4 + n + 1)
                else:
                    pe.wait_ge(a_sb, n - 1)
                if u == 0 and g % 4 == 0:
                    pe.wait_ge(a_qdup[g // 4 % 2], 16 * (b + 1))
                    if g % NG == 0:
                        pe.wait_ge(a_qlo, q_splits(b, 0))
                        pe.wait_ge(a_klo, 2 * b + 2)
                pair = 2 * (g % NG)
                if u == 0:
                    for n2 in range(2):
                        ins = nc.tensor.matmul(
                            bank[n % 2][:, n2 * S:(n2 + 1) * S].rearrange("p (h n) -> p h n", h=2),
                            qp[:, b % 2, pair + n2, 0:P], kp[:, b % 2, :, 0:P], start=True, stop=True)
                else:
                    ins = nc.tensor.matmul(bank[n % 2][:, :].rearrange("p (h n) -> p h n", h=2),
                                           qp[:, b % 2, pair + u - 1, P:S], kp[:, b % 2, :, :],
                                           start=True, stop=True)
                ins.then_inc(a_s, 1)

            def exp_transposes(n):
                pe.wait_ge(a_exp, n + 1)
                if n >= 2:
                    pe.wait_ge(a_ptc, n - 1)
                for i in range(4):
                    ins = nc.tensor.transpose(bank[2 + n % 2][:, i * P:(i + 1) * P],
                                              sc[:, n % 4, i * P:(i + 1) * P], ident[:, :])
                ins.then_inc(a_pt, 1)

            def weighted_values(g, heads):
                b = g // NG
                if heads[0] == 0:
                    if g % NG == 0:
                        pe.wait_ge(a_vp, 2 * b + 2)
                    if g >= 2:
                        pe.wait_ge(a_norm, g - 1)
                pe.wait_ge(a_ptc, 3 * g + (3 if heads[-1] >= 2 else 2))
                o = bank[4 + g % 2]
                for h in heads:
                    e = 3 * P * h
                    nc.tensor.matmul(o[0:64, 0:S], vp[:, b % 2, 0, h * 64:(h + 1) * 64], pt[:, g % 2, e:e + S],
                                     start=(h == 0), stop=False, skip_group_check=True)
                    nc.tensor.matmul(o[0:64, P:S], vp[:, b % 2, 1, h * 64:(h + 1) * 64],
                                           pt[:, g % 2, e + S:e + S + P], start=False, stop=(h == 3),
                                           skip_group_check=True)
                if heads[-1] == 3:
                    pe.wait_ge(a_inv16, g + 1)
                    for t in range(2):
                        src = inv16[:, g % 2, 4 * t:4 * t + 4, :].rearrange("p h n -> p (h n)")
                        ins = nc.tensor.transpose(o[0:64, S + t * P:S + (t + 1) * P], src, ident[:, :])
                    ins.then_inc(a_pv, 1)

            def project_out(b, t, steps):
                pe.wait_ge(a_norm, NG * (b + 1))
                for k in steps:
                    ins = nc.tensor.matmul(out_bank(b, t)[:, :], at_t[:, b % 2, k, t * P:(t + 1) * P],
                                           wo[:, k, :], start=(k == 0), stop=(k == KT - 1))
                if steps[-1] == KT - 1:
                    ins.then_inc(a_y, 1)

            def extra(m, u):
                b, g = divmod(m, NG)
                if b + 1 < B:
                    if (b >= 1 and g == 0 and u >= 1) or (m, u) == (1, 2):
                        for t in (range(2) if b == 0 else range(u - 1, u)):
                            if t == 0:
                                pe.wait_ge(a_qlo, q_splits(b, 1))
                                if b >= 2:
                                    pe.wait_ge(a_x, 2 * (b - 1))
                            transposes(tile_no("attn", b + 1, t), bank[6 + t])
                    if g == 2 and u == (1 if b == 0 else 0):
                        project_k(b + 1)
                    if g == 2 and u >= 1 and b >= 1:
                        project_v(u - 1)
                    if m == 2 and u == 2:
                        project_v(0)
                        project_v(1)
                    if g in (3, 4):
                        project_q(b + 1, g - 3, (range(0, 2), range(2, 5), range(5, 8))[u])
                elif g in (2, 4) and u == 2:
                    if g == 2:
                        pe.wait_ge(a_x, 2 * (b - 1))
                    ffn_transposes(2, g - 2)
                    ffn_transposes(2, g - 1)
                if b >= 1 and g in (6, 7):
                    if u == 0:
                        if b + 1 < B:
                            pe.wait_ge(a_qlo, q_splits(b + 1, g - 6))
                        else:
                            pe.wait_ge(xt_lo, 11 + g - 6)
                    project_out(b - 1, g - 6, (range(0, 1), range(1, 2), range(2, 4))[u])

            pe.wait_ge(consts, 1)
            for t in range(2):
                ffn_transposes(0, t)
            for t in range(2, 4):
                ffn_transposes(0, t)
            pe.wait_ge(s_first, 1)
            pe.wait_ge(z_tab, 2)
            pe.wait_ge(oh_gu, 1)
            pe.wait_ge(xt_lo, 4)
            broadcasts(0)
            broadcasts(1)
            for j in range(NJ):
                broadcasts(3 * j + 2)
                gate_up(0, j, 0)
                if j + 1 < NJ:
                    broadcasts(3 * j + 3)
                gate_up(0, j, 1)
                if j + 1 < NJ:
                    broadcasts(3 * j + 4)
                else:
                    pe.wait_ge(dq_mul, NC)
                    ffn_transposes(1, 0)
                    ffn_transposes(1, 1)
                if j >= 1:
                    down(0, j - 1)
            ffn_transposes(1, 2)
            ffn_transposes(1, 3)
            down(0, NJ - 1)
            for j in range(NJ):
                gate_up(1, j, 0)
                if j == 5:
                    for t in range(2):
                        transposes(tile_no("attn", 0, t), bank[6 + t])
                gate_up(1, j, 1)
                if j == NJ - 1:
                    pe.wait_ge(a_xt, 2)
                    pe.wait_ge(aw_in, 16 * (KT + 3))
                    project_q(0, 0, range(2 * KT))
                    project_k(0)
                    project_v(0)
                    project_v(1)
                if j >= 1:
                    down(1, j - 1)
            down(1, NJ - 1)

            pe.wait_ge(consts, 3)
            for n in range(3):
                scores(n)
                if n == 1:
                    project_q(0, 1, range(2 * KT))
            for m in range(LAST + 1):
                for u in range(3):
                    if m < LAST:
                        scores(3 * m + 3 + u)
                    exp_transposes(3 * m + u)
                    if m >= 1:
                        weighted_values(m - 1, (range(0, 2), range(2, 3), range(3, 4))[u])
                    extra(m, u)
            weighted_values(LAST, range(4))
            gate_up(2, 0, 0)
            pe.wait_ge(a_x, TT - 2)
            project_out(B - 1, 0, range(KT))
            project_out(B - 1, 1, range(KT))
            gate_up(2, 0, 1)
            for j in range(1, NJ):
                gate_up(2, j, 0)
                gate_up(2, j, 1)
                if j == NJ - 1:
                    pe.wait_ge(a_x, TT)
                    ffn_transposes(3, 0)
                    ffn_transposes(3, 1)
                down(2, j - 1)
            ffn_transposes(3, 2)
            ffn_transposes(3, 3)
            down(2, NJ - 1)
            for j in range(NJ):
                gate_up(3, j, 0)
                gate_up(3, j, 1)
                if j >= 1:
                    down(3, j - 1)
            down(3, NJ - 1)


_INS = ["L0_attn_hidden_states", "L0_attn_Wqkv", "L0_attn_Wo", "L0_ffn_qweight_gu", "L0_ffn_qzeros_gu",
        "L0_ffn_scales_gu", "L0_ffn_g_idx_gu", "L0_ffn_qweight_down", "L0_ffn_qzeros_down",
        "L0_ffn_scales_down", "L0_ffn_g_idx_down"]


def kernel(**inputs):
    import concourse.bacc as bacc
    from concourse.bass_utils import run_bass_kernel_spmd

    nc = bacc.Bacc("TRN2", target_bir_lowering=False, num_devices=1)
    arrays, args = {}, []
    for name in _INS:
        a = np.ascontiguousarray(inputs[name])
        if a.dtype == np.uint32:
            a = a.view(np.int32)
        arrays[f"in_{name}"] = a
        args.append(nc.dram_tensor(f"in_{name}", a.shape, mybir.dt.from_np(a.dtype), kind="ExternalInput").ap())
    shape = inputs["L0_attn_hidden_states"].shape
    out = nc.dram_tensor("out", shape, F32, kind="ExternalOutput").ap()
    macaron_block(nc, *args, out)
    r = run_bass_kernel_spmd(nc, [arrays], core_ids=[0])
    return r.results[0]["out"]
```
